# Optimizing a Trainium2 kernel written in Bass

```python
import numpy as np
import jax
import jax.numpy as jnp

def _softmax(x, axis=-1):
    return jax.nn.softmax(x, axis=axis)

def _gelu(x):
    return jax.nn.gelu(x, approximate=True)

def _silu(x):
    return jax.nn.silu(x)

def _sigmoid(x):
    return jax.nn.sigmoid(x)

def _layernorm(x, axis=-1, eps=1e-05):
    m = jnp.mean(x, axis=axis, keepdims=True)
    v = jnp.var(x, axis=axis, keepdims=True)
    return (x - m) / jnp.sqrt(v + eps)

def _scatter_add(tgt, idx, src, axis=0):
    return tgt.at[idx].add(src)

def _segment_sum(src, seg, n):
    return jax.ops.segment_sum(src, seg, n)
kernel_name = 'mk_gnn_preln_d2_gnn_r32_9eaa1b'

def setup_inputs(seed: int=0):
    np.random.seed(seed)
    _w = jnp.asarray

    def _rec_inputs():
        import jax
        import jax.numpy as jnp
        _gk = jax.random.key(seed)
        x = -0.0003713 + 1 * jax.random.normal(jax.random.fold_in(_gk, 1), (50000, 128), jnp.float32)
        src = jax.random.randint(jax.random.fold_in(_gk, 2), (25000,), 0, 50000, jnp.int32)
        dst = jnp.minimum((50000 * jax.random.uniform(jax.random.fold_in(_gk, 3), (25000,)) ** 2.0).astype(jnp.int32), 49999)
        _o = jnp.argsort(dst, stable=True)
        src = src[_o]
        dst = dst[_o]
        edge_weight = jax.random.uniform(jax.random.fold_in(_gk, 13), (25000,), jnp.float32, 0.0, 1)
        return (x, src, dst, edge_weight)
    x, src, dst, edge_weight = _rec_inputs()

    def _L0_gnn_setup():
        import jax, jax.numpy as jnp
        import numpy as np
        N = 3125
        E = 25000
        D = 128
        key = jax.random.key(seed)
        ks = jax.random.split(key, 12)
        s = lambda fan_in: 1.0 / np.sqrt(fan_in)
        return {'h': jax.random.normal(ks[0], (N, D), dtype=jnp.float32), 'w': jax.random.uniform(ks[1], (E,), dtype=jnp.float32), 'src': jax.random.randint(ks[2], (E,), 0, N, dtype=jnp.int32), 'dst': jax.random.randint(ks[3], (E,), 0, N, dtype=jnp.int32), 'W1': jax.random.uniform(ks[4], (2 * D + 1, D), jnp.float32, -s(2 * D + 1), s(2 * D + 1)), 'b1': jnp.zeros((D,), jnp.float32), 'W2': jax.random.uniform(ks[5], (D, D), jnp.float32, -s(D), s(D)), 'b2': jnp.zeros((D,), jnp.float32), 'U1': jax.random.uniform(ks[6], (2 * D, D), jnp.float32, -s(2 * D), s(2 * D)), 'c1': jnp.zeros((D,), jnp.float32), 'U2': jax.random.uniform(ks[7], (D, D), jnp.float32, -s(D), s(D)), 'c2': jnp.zeros((D,), jnp.float32)}
    _L0_gnn_all = _L0_gnn_setup()
    _L0_gnn_in = {k: v for k, v in _L0_gnn_all.items() if k in ('W1', 'b1', 'W2', 'b2', 'U1', 'c1', 'U2', 'c2')}
    del _L0_gnn_all

    def _L1_gnn_setup():
        import jax, jax.numpy as jnp
        import numpy as np
        N_NODES = 50000
        N_EDGES = 25000
        D_IN = 128
        D_OUT = 128
        LEAKY_SLOPE = 0.01
        BN_EPS = 1e-05
        key = jax.random.key(seed)
        k1, k2, k3, k4 = jax.random.split(key, 4)
        x = jax.random.normal(k1, (N_NODES, D_IN), dtype=jnp.float32)
        W = jax.random.normal(k2, (D_IN, D_OUT), dtype=jnp.float32) * (1.0 / np.sqrt(D_IN))
        bias = jax.random.normal(k3, (D_OUT,), dtype=jnp.float32) * 0.01
        gamma = jnp.ones((D_OUT,), dtype=jnp.float32)
        beta = jnp.zeros((D_OUT,), dtype=jnp.float32)
        edge_index = jax.random.randint(k4, (2, N_EDGES), 0, N_NODES, dtype=jnp.int32)
        return {'x': x, 'W': W, 'bias': bias, 'gamma': gamma, 'beta': beta, 'edge_index': edge_index}
    _L1_gnn_all = _L1_gnn_setup()
    _L1_gnn_in = {k: v for k, v in _L1_gnn_all.items() if k in ('W', 'bias', 'gamma', 'beta')}
    del _L1_gnn_all
    return {'x': x, 'src': src, 'dst': dst, 'edge_weight': edge_weight, 'L0_gnn_W1': _L0_gnn_in['W1'], 'L0_gnn_b1': _L0_gnn_in['b1'], 'L0_gnn_W2': _L0_gnn_in['W2'], 'L0_gnn_b2': _L0_gnn_in['b2'], 'L0_gnn_U1': _L0_gnn_in['U1'], 'L0_gnn_c1': _L0_gnn_in['c1'], 'L0_gnn_U2': _L0_gnn_in['U2'], 'L0_gnn_c2': _L0_gnn_in['c2'], 'L1_gnn_W': _L1_gnn_in['W'], 'L1_gnn_bias': _L1_gnn_in['bias'], 'L1_gnn_gamma': _L1_gnn_in['gamma'], 'L1_gnn_beta': _L1_gnn_in['beta']}

def reference(x, src, dst, edge_weight, L0_gnn_W1, L0_gnn_b1, L0_gnn_W2, L0_gnn_b2, L0_gnn_U1, L0_gnn_c1, L0_gnn_U2, L0_gnn_c2, L1_gnn_W, L1_gnn_bias, L1_gnn_gamma, L1_gnn_beta):
    import jax
    import jax.numpy as jnp

    def _L0_gnn_ref(h, w, src, dst, W1, b1, W2, b2, U1, c1, U2, c2):
        import jax, jax.numpy as jnp
        import numpy as np
        N = 3125
        E = 25000
        D = 128
        n = h.shape[0]
        msg_in = jnp.concatenate([h[src], h[dst], w[:, None]], axis=1)
        msg = jax.nn.relu(msg_in @ W1 + b1) @ W2 + b2
        agg = jax.ops.segment_max(msg, dst, num_segments=n)
        deg = jax.ops.segment_sum(jnp.ones((dst.shape[0],), jnp.int32), dst, num_segments=n)
        agg = jnp.where((deg > 0)[:, None], agg, jnp.zeros((), h.dtype))
        upd_in = jnp.concatenate([h, agg], axis=1)
        return jax.nn.relu(upd_in @ U1 + c1) @ U2 + c2

    def _L1_gnn_ref(x, W, bias, gamma, beta, edge_index):
        import jax, jax.numpy as jnp
        import numpy as np
        N_NODES = 50000
        N_EDGES = 25000
        D_IN = 128
        D_OUT = 128
        LEAKY_SLOPE = 0.01
        BN_EPS = 1e-05
        N = x.shape[0]
        loops = jnp.arange(N, dtype=edge_index.dtype)
        src = jnp.concatenate([edge_index[0], loops])
        dst = jnp.concatenate([edge_index[1], loops])
        deg = jax.ops.segment_sum(jnp.ones_like(dst, dtype=x.dtype), dst, num_segments=N)
        dinv = jnp.where(deg > 0, jax.lax.rsqrt(deg), 0.0)
        norm = dinv[src] * dinv[dst]
        h = x @ W
        msgs = h[src] * norm[:, None]
        agg = jax.ops.segment_sum(msgs, dst, num_segments=N) + bias
        a = jnp.where(agg >= 0, agg, LEAKY_SLOPE * agg)
        mean = jnp.mean(a, axis=0)
        var = jnp.var(a, axis=0)
        y = (a - mean) * jax.lax.rsqrt(var + BN_EPS) * gamma + beta
        return y
    edge_index = jnp.stack([src, dst])
    h = jnp.maximum(_layernorm(x, axis=-1), 0.0)
    x = x + _L0_gnn_ref(h, edge_weight, src, dst, L0_gnn_W1, L0_gnn_b1, L0_gnn_W2, L0_gnn_b2, L0_gnn_U1, L0_gnn_c1, L0_gnn_U2, L0_gnn_c2)
    h = jnp.maximum(_layernorm(x, axis=-1), 0.0)
    x = x + _L1_gnn_ref(h, L1_gnn_W, L1_gnn_bias, L1_gnn_gamma, L1_gnn_beta, edge_index)
    return x

_drawn_inputs = setup_inputs


def setup_inputs(seed=0):
    import zlib

    import numpy as np

    out = dict(_drawn_inputs(seed))
    spreads = {'L0_gnn_b1': (0.0, 0.8),
     'L0_gnn_b2': (0.0, 0.8),
     'L0_gnn_c1': (0.0, 0.1),
     'L0_gnn_c2': (0.0, 0.1),
     'L1_gnn_gamma': (1.0, 0.2),
     'L1_gnn_beta': (0.0, 0.1)}
    factors = {'edge_weight': 8.0, 'L0_gnn_W1': 4.778, 'L0_gnn_W2': 3.827, 'L1_gnn_bias': 6.759}
    for name, (base, spread) in spreads.items():
        noise = np.random.default_rng([zlib.crc32(name.encode()), seed]).standard_normal(out[name].shape)
        drawn = base * np.exp(spread * noise) if base else spread * noise
        out[name] = jnp.asarray(drawn.astype(out[name].dtype))
    for name, factor in factors.items():
        out[name] = (out[name] * factor).astype(out[name].dtype)
    return out
```

```python
from contextlib import ExitStack

import concourse.bass as bass
from concourse import mybir

F32 = mybir.dt.float32
I32 = mybir.dt.int32
ALU = mybir.AluOpType
ACT = mybir.ActivationFunctionType

P = 128
D = 128
J = 4
G = P * J
LN_EPS = 1e-5
BN_EPS = 1e-5
SLOPE = 0.01
AW = D + 1
XW = D + 2
RESTART = 1e30


def gnn_kernel(nc, x, src, dst, w, W1, b1, W2, b2, U1, c1, U2, c2, W, bias, gamma, beta, out):
    N = x.shape[0]
    E = src.shape[0]
    EG = -(-E // G)
    ET = EG * J
    NG = -(-N // G)
    LAST_BASE = N - G
    DOUBLE = ((NG - 1) * G - LAST_BASE) // J
    assert NG == 2 * EG and EG % 2 == 1 and ((NG - 1) * G - LAST_BASE) % J == 0
    EC = 2 * P
    EQ = EG * G // EC
    EFULL = E // EC
    EREST = E - EFULL * EC
    assert EQ == EFULL + 1 and EREST > 1
    NOWHERE = 2 * N
    ZC = 25
    ZP = 80
    ZN = N * AW // (ZC * ZP)
    assert ZN * ZC * ZP == N * AW

    agg_d = nc.dram_tensor("agg_d", (N, AW), F32, kind="Internal").ap()
    x1_d = nc.dram_tensor("x1_d", (N, XW), F32, kind="Internal").ap()
    z0_d = nc.dram_tensor("z0_d", (NG * P, G), F32, kind="Internal").ap()
    pre_d = nc.dram_tensor("pre_d", (NG * P, G), F32, kind="Internal").ap()
    act_d = nc.dram_tensor("act_d", (NG * P, G), F32, kind="Internal").ap()
    pen_d = nc.dram_tensor("pen_d", (EG, G), F32, kind="Internal").ap()
    keep_d = nc.dram_tensor("keep_d", (EG, G), F32, kind="Internal").ap()
    w_d = nc.dram_tensor("w_d", (EG, G), F32, kind="Internal").ap()

    def rows(table, t, width):
        if isinstance(t, int):
            base = min(t * G, LAST_BASE)
            part = table[base:base + G, 0:width]
        else:
            part = table[bass.ds(t * G, G), 0:width]
        return part.rearrange("(p j) f -> p (j f)", j=J)

    def block_rows(table, t):
        return table[bass.ds(t * P, P), :] if not isinstance(t, int) else table[t * P:(t + 1) * P, :]

    def cols(t, n):
        return bass.ds(t * n, n) if not isinstance(t, int) else slice(t * n, (t + 1) * n)

    ctx = ExitStack()
    with ctx:
        def sb(name, shape, dt=F32):
            return ctx.enter_context(nc.sbuf_tensor(name, shape, dt))

        def sem(name):
            return ctx.enter_context(nc.semaphore(name))

        def sems(name, n=2):
            return [sem(f"{name}{k}") for k in range(n)]

        ident = sb("ident", [P, P])
        ones_row = sb("ones_row", [1, P])
        w1a, w1b, w2 = sb("w1a", [P, D]), sb("w1b", [P, D]), sb("w2", [P, D])
        u1a, u1b, u2, wg = sb("u1a", [P, D]), sb("u1b", [P, D]), sb("u2", [P, D]), sb("wg", [P, D])
        w1w = sb("w1w", [1, D])
        b1c, b2c, c1c, biasc = sb("b1c", [P, 1]), sb("b2c", [P, 1]), sb("c1c", [P, 1]), sb("biasc", [P, 1])
        gammac, betac = sb("gammac", [P, 1]), sb("betac", [P, 1])
        eps_col, one_col = sb("eps_col", [P, 1]), sb("one_col", [P, 1])
        c2_bc = sb("c2_bc", [P, G])
        src_t, dst_t, put_t = sb("src_t", [P, ET], I32), sb("dst_t", [P, ET], I32), sb("put_t", [P, ET], I32)
        count_t, dinv_t = sb("count_t", [P, ET]), sb("dinv_t", [P, ET])
        dinv_n = sb("dinv_n", [P, NG * J])
        stats_n = sb("stats_n", [P, NG, 6])
        def ring(name, shape, dt=F32):
            return [sb(f"{name}{k}", shape, dt) for k in range(2)]

        xg = ring("xg", [P, 8 * XW])
        hs, hd = ring("hs", [P, G]), ring("hd", [P, G])
        ze, ms = ring("ze", [P, G]), ring("ms", [P, G])
        scan = ring("scan", [P, G])
        keepb = ring("keepb", [P, G])
        wrow = ring("wrow", [1, G])
        gr = ring("gr", [P, J * AW])
        get_idx = ring("get_idx", [P, 8], I32)
        put_idx = ring("put_idx", [P, J], I32)
        xn = ring("xn", [P, J * XW])
        hn, zn = ring("hn", [P, G]), ring("zn", [P, G])
        gn = ring("gn", [P, J * AW])
        xc = ring("xc", [P, G])
        st = ring("st", [P, 16, 6])
        mv = ring("mv", [P, 16, 2])
        sd = ring("sd", [P, 16])
        rs = ring("rs", [P, 16])

        bank = [ctx.enter_context(nc.psum_tensor(f"bank{k}", [P, 512], F32)) for k in range(8)]

        dst_a, prev_a, next_a, src_a = (sb(n, [P, EC], I32) for n in ("dst_a", "prev_a", "next_a", "src_a"))
        w_a = sb("w_a", [P, EC])
        pen_a, keep_a, local_a, allkeep_a, count_a, put_a = (
            sb(n, [P, EC]) for n in ("pen_a", "keep_a", "local_a", "allkeep_a", "count_a", "put_a"))
        srcf_a, dstf_a, same_a = sb("srcf_a", [P, EC]), sb("dstf_a", [P, EC]), sb("same_a", [P, EC])
        ones_a, zeros_a = sb("ones_a", [P, EC]), sb("zeros_a", [P, EC])
        ends_r = sb("ends_r", [1, 2 * EQ])
        carry_r = sb("carry_r", [1, EQ + 1])
        carry_c = sb("carry_c", [P, 1])
        zero_t = sb("zero_t", [ZP, ZN])

        s_blank = sem("s_blank")
        s_fill = sem("s_fill")
        s_weights = sem("s_weights")
        s_edges = sem("s_edges")
        s_zero = sem("s_zero")
        s_agg0 = sem("s_agg0")
        s_id = sem("s_id")
        s_arr = sem("s_arr")
        s_ends = sem("s_ends")
        s_carry = sem("s_carry")
        s_tr = sem("s_tr")
        s_tv = sem("s_tv")
        s_dv = sem("s_dv")
        s_masks = sem("s_masks")

        def col(v):
            return v.rearrange("(p o) -> p o", o=1)

        weight_loads = [
            (w1a[:, :], W1[0:D, :]), (w1b[:, :], W1[D:2 * D, :]), (w1w[:, :], W1[2 * D:2 * D + 1, :]),
            (w2[:, :], W2[:, :]), (u1a[:, :], U1[0:D, :]), (u1b[:, :], U1[D:2 * D, :]),
            (u2[:, :], U2[:, :]), (wg[:, :], W[:, :]),
            (b1c[:, :], col(b1)), (b2c[:, :], col(b2)), (c1c[:, :], col(c1)), (biasc[:, :], col(bias)),
            (gammac[:, :], col(gamma)), (betac[:, :], col(beta)),
        ] + [(c2_bc[:, j * D:(j + 1) * D], c2.rearrange("(o f) -> o f", o=1).to_broadcast([P, D]))
             for j in range(J)]
        N_WEIGHTS = len(weight_loads)

        with nc.Block() as block:
            @block.gpsimd
            def _(g):
                g.memset(dst_a[:, :], N).then_inc(s_blank, 1)
                g.memset(prev_a[:, :], -1).then_inc(s_blank, 1)
                g.memset(next_a[:, :], N).then_inc(s_blank, 1)
                g.memset(src_a[:, :], 0).then_inc(s_blank, 1)
                g.memset(w_a[:, :], 0.0).then_inc(s_blank, 1)
                g.memset(zero_t[:, :], 0.0).then_inc(s_zero, 1)
                g.memset(ident[:, :], 0.0).then_inc(s_id, 1)
                g.wait_ge(s_id, 1)
                g.affine_select(out=ident[:, :], in_=ident[:, :], compare_op=ALU.not_equal, fill=1.0,
                                base=0, pattern=[[-1, P]], channel_multiplier=1).then_inc(s_id, 1)

            @block.sync
            def _(sp):
                def flat(v, a, b):
                    return v[a:b].rearrange("(q c) -> q c", c=EC)

                def line(v, a, b):
                    return v[a:b].rearrange("(q c) -> q c", q=1)

                sp.wait_ge(s_blank, 5)
                full = EFULL * EC
                for tile, v in ((dst_a, dst), (src_a, src), (w_a, w)):
                    sp.dma_start(tile[0:EFULL, :], flat(v, 0, full)).then_inc(s_edges, 16)
                    sp.dma_start(tile[EFULL:EQ, 0:EREST], line(v, full, E)).then_inc(s_edges, 16)
                sp.dma_start(prev_a[0:1, 1:EC], line(dst, 0, EC - 1)).then_inc(s_edges, 16)
                sp.dma_start(prev_a[1:EFULL, :], flat(dst, EC - 1, full - 1)).then_inc(s_edges, 16)
                sp.dma_start(prev_a[EFULL:EQ, 0:EREST], line(dst, full - 1, E - 1)).then_inc(s_edges, 16)
                sp.dma_start(next_a[0:EFULL, :], flat(dst, 1, full + 1)).then_inc(s_edges, 16)
                sp.dma_start(next_a[EFULL:EQ, 0:EREST - 1], line(dst, full + 1, E)).then_inc(s_edges, 16)
                sp.wait_ge(s_edges, 16 * 11)
                sp.dma_start(w_d.rearrange("s (h c) -> (s h) c", c=EC), w_a[0:EQ, :]).then_inc(s_masks, 16)
                sp.wait_ge(s_arr, 2)
                sp.dma_start(pen_d.rearrange("s (h c) -> (s h) c", c=EC), pen_a[0:EQ, :]).then_inc(s_masks, 16)
                sp.dma_start(keep_d.rearrange("s (h c) -> (s h) c", c=EC), keep_a[0:EQ, :]).then_inc(s_masks, 16)
                sp.wait_ge(s_masks, 48)
                sp.wait_ge(s_weights, 16 * N_WEIGHTS)

            @block.scalar
            def _(act):
                for to, of in weight_loads:
                    act.dma_start(to, of).then_inc(s_weights, 16)
                act.wait_ge(s_zero, 1)
                zeros = agg_d.rearrange("n a -> (n a)").rearrange("(k z c) -> k z c", z=ZP, c=ZN)
                for k in range(ZC):
                    act.dma_start(zeros[k, :, :], zero_t[:, :]).then_inc(s_agg0, 16)
                act.wait_ge(s_tv, 4)
                act.wait_ge(s_arr, 12)
                nc.scalar.activation(dinv_t[:, :], count_t[:, :], ACT.Sqrt, bias=one_col[:, :]).then_inc(s_dv, 1)

            @block.vector
            def _(dve):
                v = nc.vector
                v.memset(ones_a[:, :], 1.0).then_inc(s_fill, 1)
                v.memset(zeros_a[:, :], 0.0).then_inc(s_fill, 1)
                v.memset(eps_col[:, :], LN_EPS).then_inc(s_fill, 1)
                v.memset(one_col[:, :], 1.0).then_inc(s_fill, 1)
                v.memset(ones_row[:, :], 1.0).then_inc(s_fill, 1)
                v.memset(carry_r[:, :], 0.0).then_inc(s_fill, 1)
                dve.wait_ge(s_edges, 16 * 11)
                dve.wait_ge(s_fill, 6)
                q = slice(0, EQ)
                v.tensor_tensor(same_a[q, :], prev_a[q, :], dst_a[q, :], ALU.subtract).then_inc(s_dv, 1)
                dve.wait_ge(s_dv, 1)
                v.tensor_scalar(pen_a[q, :], same_a[q, :], RESTART, None, ALU.mult).then_inc(s_arr, 1)
                v.tensor_scalar(keep_a[q, :], same_a[q, :], 0.0, None, ALU.is_equal).then_inc(s_arr, 1)
                dve.wait_ge(s_arr, 2)
                v.tensor_tensor_scan(local_a[q, :], keep_a[q, :], ones_a[q, :], 0.0, ALU.mult, ALU.add).then_inc(s_arr, 1)
                v.tensor_tensor_scan(allkeep_a[q, :], keep_a[q, :], zeros_a[q, :], 1.0, ALU.mult, ALU.add).then_inc(s_arr, 1)
                v.tensor_copy(srcf_a[q, :], src_a[q, :]).then_inc(s_arr, 1)
                v.tensor_copy(dstf_a[q, :], dst_a[q, :]).then_inc(s_arr, 1)
                v.tensor_copy(count_a[q, :], next_a[q, :]).then_inc(s_arr, 1)
                dve.wait_ge(s_arr, 7)
                v.tensor_tensor(same_a[q, :], count_a[q, :], dstf_a[q, :], ALU.is_equal).then_inc(s_arr, 1)
                dve.wait_ge(s_arr, 8)
                v.scalar_tensor_tensor(out=put_a[q, :], in0=same_a[q, :], scalar=float(NOWHERE), in1=dstf_a[q, :],
                                       op0=ALU.mult, op1=ALU.add).then_inc(s_arr, 1)
                dve.wait_ge(s_ends, 1)
                v.tensor_copy(ends_r[:, :], bank[0][0:1, 0:2 * EQ]).then_inc(s_arr, 1)
                dve.wait_ge(s_arr, 10)
                v.tensor_tensor_scan(carry_r[:, 1:EQ + 1], ends_r[:, EQ:2 * EQ], ends_r[:, 0:EQ], 0.0,
                                     ALU.mult, ALU.add).then_inc(s_arr, 1)
                dve.wait_ge(s_carry, 1)
                v.tensor_copy(carry_c[q, :], bank[1][q, 0:1]).then_inc(s_dv, 1)
                dve.wait_ge(s_dv, 2)
                v.scalar_tensor_tensor(out=count_a[q, :], in0=allkeep_a[q, :], scalar=carry_c[q, :], in1=local_a[q, :],
                                       op0=ALU.mult, op1=ALU.add).then_inc(s_arr, 1)
                for k, to in enumerate((src_t, dst_t, put_t, count_t)):
                    dve.wait_ge(s_tr, k + 1)
                    v.tensor_copy(to[:, :].rearrange("p (q h) -> p h q", h=2),
                                  bank[2 + k][:, 0:2 * EQ].rearrange("p (h q) -> p h q", h=2)).then_inc(s_tv, 1)
                dve.wait_ge(s_dv, 3)
                v.reciprocal(dinv_t[:, :], dinv_t[:, :]).then_inc(s_dv, 1)

            @block.tensor
            def _(pe):
                pe.wait_ge(s_id, 2)
                pe.wait_ge(s_arr, 4)
                for k, of in enumerate((local_a, allkeep_a)):
                    last = nc.tensor.matmul(bank[0][0:1, k * EQ:(k + 1) * EQ], of[0:EQ, EC - 1:EC],
                                            ident[0:EQ, 0:EQ], start=True, stop=True)
                last.then_inc(s_ends, 1)
                pe.wait_ge(s_arr, 11)
                nc.tensor.matmul(bank[1][0:EQ, 0:1], carry_r[:, 0:EQ], ones_row[:, 0:1],
                                 start=True, stop=True).then_inc(s_carry, 1)
                for k, of in enumerate((srcf_a, dstf_a, put_a, count_a)):
                    if k == 3:
                        pe.wait_ge(s_arr, 12)
                    for h in range(2):
                        last = nc.tensor.transpose(bank[2 + k][:, h * EQ:(h + 1) * EQ],
                                                   of[0:EQ, h * P:(h + 1) * P], ident[0:EQ, 0:EQ])
                    last.then_inc(s_tr, 1)

        def wait(eng, signal, value):
            if not isinstance(value, int) or value > 0:
                eng.wait_ge(signal, value)

        def hold(eng, signal, value):
            if not isinstance(value, int) or value > 0:
                eng.wait_ge(signal, value)
                eng.sem_inc(s_held, 1)

        def steps(eng, n, step):
            for i in range(4):
                step(i, i % 2, i // 2)
            with eng.Fori(2, (n - 1) // 2) as h:
                step(2 * h, 0, h)
                step(2 * h + 1, 1, h)
            for i in range((n - 1) // 2 * 2, n):
                step(i, i % 2, i // 2)

        def before(i, k, h):
            return i - 1, 1 - k, h - 1 + k

        s_held = sem("s_held")
        v = nc.vector

        a_get = sems("a_get")
        a_mask = sems("a_mask")
        a_put = sems("a_put")
        a_x = sems("a_x")
        a_z = sems("a_z")
        a_gi, a_pi = sem("a_gi"), sem("a_pi")
        a_st, a_agg, a_std, a_rs = (sem("a_" + n) for n in ("st", "agg", "std", "rs"))
        a_norm = sem("a_norm")
        a_tr = sem("a_tr")
        a_relu = sem("a_relu")
        a_hid = sem("a_hid")
        a_ze = sem("a_ze")
        a_msg = sem("a_msg")
        a_ms = sem("a_ms")
        a_scan = sem("a_scan")
        a_gu = sem("a_gu")
        a_gr = sem("a_gr")
        a_nnorm, a_ntr, a_nrelu = sem("a_nnorm"), sem("a_ntr"), sem("a_nrelu")
        a_nz = sem("a_nz")
        a_nzs = sem("a_nzs")
        T0, T1, BZ, BM, BG, BD, BN = bank[0:7]

        with nc.Block() as block:
            @block.gpsimd
            def _(g):
                def gather(i, k, h):
                    hold(g, a_tr, i - 1)
                    g.tensor_copy(get_idx[k][:, 0:J], src_t[:, cols(i, J)]).then_inc(a_gi, 1)
                    g.tensor_copy(get_idx[k][:, J:2 * J], dst_t[:, cols(i, J)]).then_inc(a_gi, 1)
                    hold(g, a_gi, 2 * i + 2)
                    for j in range(2 * J):
                        g.indirect_dma_start(
                            out=xg[k][:, j * D:(j + 1) * D], out_offset=None, in_=x[:, :],
                            in_offset=bass.IndirectOffsetOnAxis(ap=get_idx[k][:, j:j + 1], axis=0),
                            bounds_check=N - 1, oob_is_err=False).then_inc(a_get[k], 16)

                def scatter(i, k, h):
                    hold(g, a_put[k], 64 * h)
                    g.tensor_copy(put_idx[k][:, :], put_t[:, cols(i, J)]).then_inc(a_pi, 1)
                    hold(g, a_pi, i + 1)
                    hold(g, a_gr, i + 1)
                    for j in range(J):
                        g.indirect_dma_start(
                            out=agg_d[:, :], in_=gr[k][:, j * AW:(j + 1) * AW],
                            out_offset=bass.IndirectOffsetOnAxis(ap=put_idx[k][:, j:j + 1], axis=0),
                            in_offset=None, bounds_check=N - 1, oob_is_err=False).then_inc(a_put[k], 16)

                def step(i, k, h):
                    gather(i, k, h)
                    if isinstance(i, int) and i < 2:
                        return
                    if isinstance(i, int) and i == 2:
                        g.wait_ge(s_agg0, 16 * ZC)
                    scatter(i - 2, k, h - 1)
                steps(g, EG, step)
                for i in range(EG - 2, EG):
                    scatter(i, i % 2, i // 2)
                for k in range(2):
                    g.wait_ge(a_put[k], 64 * ((EG + 1 - k) // 2))

            @block.sync
            def _(sp):
                def step(i, k, h):
                    wait(sp, a_scan, i - 1)
                    sp.dma_start(keepb[k][:, :], pen_d[cols(i, 1), :].to_broadcast([P, G])).then_inc(a_mask[k], 16)
                    wait(sp, a_hid, i - 1)
                    sp.dma_start(wrow[k][:, :], w_d[cols(i, 1), :]).then_inc(a_mask[k], 16)
                    for d in range(2):
                        wait(sp, a_ntr, 2 * i + d - 1)
                        t = 2 * i + d
                        sp.dma_start(xn[d][:, 0:G], rows(x, t, D)).then_inc(a_x[d], 16)
                steps(sp, EG, step)

            @block.vector
            def _(dve):
                def scan_step(i, k, h):
                    wait(dve, a_ms, i + 1)
                    wait(dve, a_mask[k], 32 * h + 32)
                    wait(dve, a_gu, i - 1)
                    wait(dve, a_scan, i)
                    v.tensor_tensor_scan(
                        scan[k][:, :], keepb[k][:, :], ms[k][:, :],
                        -RESTART if isinstance(i, int) and i == 0 else scan[1 - k][:, G - 1:G],
                        ALU.add, ALU.max).then_inc(a_scan, 1)

                def step(i, k, h):
                    wait(dve, a_get[k], 128 * h + 128)
                    for j in range(8):
                        v.bn_stats(st[k][:, j, :], xg[k][:, j * D:(j + 1) * D])
                    for d in range(2):
                        wait(dve, a_x[d], 16 * i + 16)
                        for j in range(J):
                            last = v.bn_stats(st[k][:, 8 + J * d + j, :], xn[d][:, j * D:(j + 1) * D])
                    last.then_inc(a_st, 1)
                    hold(dve, a_st, i + 1)
                    for j in range(16):
                        last = v.bn_aggr(mv[k][:, j, :], st[k][:, j, :])
                    last.then_inc(a_agg, 1)
                    if not isinstance(i, int) or i:
                        scan_step(*before(i, k, h))
                    wait(dve, a_std, i + 1)
                    v.reciprocal(rs[k][:, :], sd[k][:, :]).then_inc(a_rs, 1)
                    wait(dve, a_rs, i + 1)
                    for j in range(8):
                        row = xg[k][:, j * D:(j + 1) * D]
                        last = v.tensor_scalar(row, row, mv[k][:, j, 0:1], rs[k][:, j:j + 1],
                                               ALU.subtract, ALU.mult)
                    last.then_inc(a_norm, 1)
                    for d in range(2):
                        for j in range(J):
                            row, m = xn[d][:, j * D:(j + 1) * D], 8 + J * d + j
                            last = v.tensor_scalar(row, row, mv[k][:, m, 0:1], rs[k][:, m:m + 1],
                                                   ALU.subtract, ALU.mult)
                        last.then_inc(a_nnorm, 1)
                steps(dve, EG, step)
                scan_step(EG - 1, (EG - 1) % 2, (EG - 1) // 2)

            @block.scalar
            def _(act):
                s = nc.scalar

                def rows_out(i, k, h):
                    wait(act, a_gu, i + 1)
                    wait(act, a_put[k], 64 * h)
                    s.activation(gr[k][:, :].rearrange("p (j a) -> p j a", a=AW)[:, :, 0:D],
                                 BG[:, :].rearrange("p (j f) -> p j f", f=D), ACT.Copy)
                    s.activation(gr[k][:, :].rearrange("p (j a) -> p j a", a=AW)[:, :, D],
                                 count_t[:, cols(i, J)], ACT.Copy).then_inc(a_gr, 1)

                def node_relu(i, d):
                    wait(act, a_ntr, 2 * i + d + 1)
                    wait(act, a_nz, 2 * i + d - 1)
                    s.activation(hn[d][:, :], BD[:, :], ACT.Relu).then_inc(a_nrelu, 1)

                def node_out(i, d):
                    wait(act, a_nz, 2 * i + d + 1)
                    wait(act, a_z[d], 16 * i)
                    s.activation(zn[d][:, :], BN[:, :], ACT.Identity, bias=c1c[:, :]).then_inc(a_nzs, 1)
                    wait(act, a_nzs, 2 * i + d + 1)
                    act.dma_start(block_rows(z0_d, 2 * i + d), zn[d][:, :]).then_inc(a_z[d], 16)

                def step(i, k, h):
                    wait(act, a_agg, i + 1)
                    wait(act, a_rs, i - 1)
                    s.activation(sd[k][:, :], mv[k][:, :, 1], ACT.Sqrt, bias=eps_col[:, :]).then_inc(a_std, 1)
                    if not isinstance(i, int) or i:
                        rows_out(*before(i, k, h))
                    wait(act, a_tr, i + 1)
                    wait(act, a_hid, i - 1)
                    s.activation(hs[k][:, :], T0[:, :], ACT.Relu)
                    s.activation(hd[k][:, :], T1[:, :], ACT.Relu).then_inc(a_relu, 1)
                    node_relu(i, 0)
                    wait(act, a_hid, i + 1)
                    wait(act, a_msg, i - 1)
                    s.activation(ze[k][:, :], BZ[:, :], ACT.Relu, bias=b1c[:, :]).then_inc(a_ze, 1)
                    node_out(i, 0)
                    node_relu(i, 1)
                    wait(act, a_msg, i + 1)
                    wait(act, a_scan, i - 1)
                    s.activation(ms[k][:, :], BM[:, :], ACT.Identity, bias=b2c[:, :]).then_inc(a_ms, 1)
                    node_out(i, 1)
                steps(act, EG, step)
                rows_out(EG - 1, (EG - 1) % 2, (EG - 1) // 2)
                for d in range(2):
                    act.wait_ge(a_z[d], 16 * EG)

            @block.tensor
            def _(pe):
                mm = nc.tensor.matmul

                def times_u1(i, k, h):
                    wait(pe, a_scan, i + 1)
                    wait(pe, a_gr, i)
                    for j in range(J):
                        last = mm(BG[:, j * D:(j + 1) * D], scan[k][:, j * P:(j + 1) * P], u1b[:, :],
                                  start=True, stop=True)
                    last.then_inc(a_gu, 1)

                def node_transpose(i, d):
                    wait(pe, a_nnorm, 2 * i + d + 1)
                    wait(pe, a_nrelu, 2 * i + d)
                    for j in range(J):
                        last = nc.tensor.transpose(BD[:, j * P:(j + 1) * P], xn[d][:, j * D:(j + 1) * D], ident[:, :])
                    last.then_inc(a_ntr, 1)

                def node_times_u1(i, d):
                    wait(pe, a_nrelu, 2 * i + d + 1)
                    wait(pe, a_nzs, 2 * i + d)
                    mm(BN[:, :], u1a[:, :], hn[d][:, :], start=True, stop=True).then_inc(a_nz, 1)

                def step(i, k, h):
                    if not isinstance(i, int) or i:
                        times_u1(*before(i, k, h))
                    wait(pe, a_norm, i + 1)
                    wait(pe, a_relu, i)
                    for j in range(J):
                        nc.tensor.transpose(T0[:, j * P:(j + 1) * P], xg[k][:, j * D:(j + 1) * D], ident[:, :])
                    for j in range(J):
                        last = nc.tensor.transpose(T1[:, j * P:(j + 1) * P], xg[k][:, (J + j) * D:(J + j + 1) * D],
                                                   ident[:, :])
                    last.then_inc(a_tr, 1)
                    node_transpose(i, 0)
                    wait(pe, a_relu, i + 1)
                    wait(pe, a_mask[k], 32 * h + 32)
                    wait(pe, a_ze, i)
                    mm(BZ[:, :], w1a[:, :], hs[k][:, :], start=True, stop=False)
                    mm(BZ[:, :], w1b[:, :], hd[k][:, :], start=False, stop=False)
                    mm(BZ[:, :], w1w[:, :], wrow[k][:, :], start=False, stop=True).then_inc(a_hid, 1)
                    node_times_u1(i, 0)
                    node_transpose(i, 1)
                    wait(pe, a_ze, i + 1)
                    wait(pe, a_ms, i)
                    mm(BM[:, :], w2[:, :], ze[k][:, :], start=True, stop=True).then_inc(a_msg, 1)
                    node_times_u1(i, 1)
                steps(pe, EG, step)
                times_u1(EG - 1, (EG - 1) % 2, (EG - 1) // 2)

        u_ld = sems("u_ld")
        u_st = sems("u_st")
        u_xc = sem("u_xc")
        u_pre = sem("u_pre")
        u_relu = sem("u_relu")
        u_cnt = sem("u_cnt")
        u_out = sem("u_out")
        u_x1 = sem("u_x1")
        u_sts, u_agg, u_std = sem("u_sts"), sem("u_agg"), sem("u_std")
        u_rs = sem("u_rs")
        u_fin = sem("u_fin")
        BA, BX = bank[0:2], bank[2:4]

        with nc.Block() as block:
            @block.sync
            def _(sp):
                def step(t, k, h):
                    wait(sp, u_pre, t - 1)
                    wait(sp, u_cnt, t - 1)
                    sp.dma_start(gn[k][:, :], rows(agg_d, t, AW)).then_inc(u_ld[k], 16)
                    sp.dma_start(hn[k][:, :], block_rows(z0_d, t)).then_inc(u_ld[k], 16)
                    wait(sp, u_x1, t - 1)
                    sp.dma_start(xc[k][:, :], rows(x, t, D)).then_inc(u_ld[k], 16)
                steps(sp, NG, step)

            @block.gpsimd
            def _(g):
                def step(t, k, h):
                    wait(g, u_ld[k], 48 * h + 48)
                    g.tensor_tensor(xc[k][:, :], xc[k][:, :], c2_bc[:, :], ALU.add).then_inc(u_xc, 1)
                steps(g, NG, step)

            @block.tensor
            def _(pe):
                mm = nc.tensor.matmul

                def times_u2(t, k, h):
                    wait(pe, u_relu, t + 1)
                    wait(pe, u_x1, t - 1)
                    for j in range(J):
                        last = mm(BX[k][:, j * D:(j + 1) * D], zn[k][:, j * P:(j + 1) * P], u2[:, :],
                                  start=True, stop=True)
                    last.then_inc(u_out, 1)

                def step(t, k, h):
                    wait(pe, u_ld[k], 48 * h + 48)
                    wait(pe, u_relu, t - 1)
                    mm(BA[k][:, :], ident[:, :], hn[k][:, :], start=True, stop=False)
                    for j in range(J):
                        last = mm(BA[k][:, j * P:(j + 1) * P], gn[k][:, j * AW:j * AW + D], ident[:, :],
                                  start=False, stop=j == J - 1)
                    last.then_inc(u_pre, 1)
                    if not isinstance(t, int) or t:
                        times_u2(*before(t, k, h))
                steps(pe, NG, step)
                times_u2(NG - 1, (NG - 1) % 2, (NG - 1) // 2)

            @block.scalar
            def _(act):
                s = nc.scalar

                def deviation(t, k, h):
                    wait(act, u_agg, t + 1)
                    s.activation(sd[k][:, 0:J], xn[k][:, :].rearrange("p (j a) -> p j a", a=XW)[:, :, D + 1],
                                 ACT.Sqrt, bias=eps_col[:, :]).then_inc(u_std, 1)

                def store(t, k, h):
                    wait(act, u_fin, t + 1)
                    if isinstance(t, int) and t == NG - 1:
                        act.wait_ge(u_st[1 - k], 16 * (NG // 2))
                    act.dma_start(rows(x1_d, t, XW), xn[k][:, :]).then_inc(u_st[k], 16)

                def step(t, k, h):
                    wait(act, u_pre, t + 1)
                    wait(act, u_out, t - 1)
                    s.activation(zn[k][:, :], BA[k][:, :], ACT.Relu).then_inc(u_relu, 1)
                    if not isinstance(t, int) or t >= 2:
                        store(t - 2, k, h - 1)
                    s.activation(sd[k][:, J:2 * J], gn[k][:, :].rearrange("p (j a) -> p j a", a=AW)[:, :, D],
                                 ACT.Sqrt, bias=one_col[:, :]).then_inc(u_cnt, 1)
                    if not isinstance(t, int) or t:
                        deviation(*before(t, k, h))
                steps(act, NG, step)
                deviation(NG - 1, (NG - 1) % 2, (NG - 1) // 2)
                for t in (NG - 2, NG - 1):
                    store(t, t % 2, t // 2)
                for k in range(2):
                    act.wait_ge(u_st[k], 16 * (NG // 2))

            @block.vector
            def _(dve):
                def add_x(t, k, h):
                    wait(dve, u_out, t + 1)
                    wait(dve, u_xc, t + 1)
                    wait(dve, u_st[k], 16 * h)
                    x1 = xn[k][:, :].rearrange("p (j a) -> p j a", a=XW)
                    v.tensor_tensor(x1[:, :, 0:D], BX[k][:, :].rearrange("p (j f) -> p j f", f=D),
                                    xc[k][:, :].rearrange("p (j f) -> p j f", f=D), ALU.add).then_inc(u_x1, 1)
                    wait(dve, u_x1, t + 1)
                    for j in range(J):
                        last = v.bn_stats(st[k][:, j, :], x1[:, j, 0:D])
                    last.then_inc(u_sts, 1)
                    hold(dve, u_sts, t + 1)
                    for j in range(J):
                        last = v.bn_aggr(x1[:, j, D:XW], st[k][:, j, :])
                    last.then_inc(u_agg, 1)

                def scales(t, k, h):
                    wait(dve, u_std, t + 1)
                    wait(dve, u_cnt, t + 1)
                    v.reciprocal(rs[k][:, 0:J], sd[k][:, 0:J])
                    v.reciprocal(dinv_n[:, cols(t, J)], sd[k][:, J:2 * J]).then_inc(u_rs, 1)
                    wait(dve, u_rs, t + 1)
                    x1 = xn[k][:, :].rearrange("p (j a) -> p j a", a=XW)
                    v.tensor_tensor(x1[:, :, D + 1], rs[k][:, 0:J], dinv_n[:, cols(t, J)], ALU.mult).then_inc(u_fin, 1)

                def step(t, k, h):
                    if not isinstance(t, int) or t >= 2:
                        scales(t - 2, k, h - 1)
                    if not isinstance(t, int) or t:
                        add_x(*before(t, k, h))
                steps(dve, NG, step)
                scales(NG - 2, NG % 2, NG // 2 - 1)
                add_x(NG - 1, (NG - 1) % 2, (NG - 1) // 2)
                scales(NG - 1, (NG - 1) % 2, (NG - 1) // 2)

        b_get, b_mask, b_put, b_x, b_z = (sems("b_" + n) for n in ("get", "mask", "put", "x", "z"))
        b_gi, b_pi = sem("b_gi"), sem("b_pi")
        b_norm, b_tr, b_relu = sem("b_norm"), sem("b_tr"), sem("b_relu")
        b_scan = sem("b_scan")
        b_gw = sem("b_gw")
        b_gr = sem("b_gr")
        b_sc = sem("b_sc")
        b_nnorm, b_ntr, b_nrelu, b_nz, b_nzs = (sem("b_" + n) for n in ("nnorm", "ntr", "nrelu", "nz", "nzs"))

        with nc.Block() as block:
            @block.gpsimd
            def _(g):
                def gather(i, k, h):
                    hold(g, b_tr, i - 1)
                    g.tensor_copy(get_idx[k][:, 0:J], src_t[:, cols(i, J)]).then_inc(b_gi, 1)
                    hold(g, b_gi, i + 1)
                    for j in range(J):
                        g.indirect_dma_start(
                            out=xg[k][:, j * XW:(j + 1) * XW], out_offset=None, in_=x1_d[:, :],
                            in_offset=bass.IndirectOffsetOnAxis(ap=get_idx[k][:, j:j + 1], axis=0),
                            bounds_check=N - 1, oob_is_err=False).then_inc(b_get[k], 16)

                def scatter(i, k, h):
                    hold(g, b_put[k], 64 * h)
                    g.tensor_copy(put_idx[k][:, :], put_t[:, cols(i, J)]).then_inc(b_pi, 1)
                    hold(g, b_pi, i + 1)
                    hold(g, b_gr, i + 1)
                    for j in range(J):
                        g.indirect_dma_start(
                            out=agg_d[:, :], in_=gr[k][:, j * AW:(j + 1) * AW],
                            out_offset=bass.IndirectOffsetOnAxis(ap=put_idx[k][:, j:j + 1], axis=0),
                            in_offset=None, bounds_check=N - 1, oob_is_err=False).then_inc(b_put[k], 16)

                def step(i, k, h):
                    gather(i, k, h)
                    if not isinstance(i, int) or i >= 2:
                        scatter(i - 2, k, h - 1)
                steps(g, EG, step)
                for i in range(EG - 2, EG):
                    scatter(i, i % 2, i // 2)
                for k in range(2):
                    g.wait_ge(b_put[k], 64 * ((EG + 1 - k) // 2))

            @block.sync
            def _(sp):
                def step(i, k, h):
                    wait(sp, b_scan, i - 1)
                    sp.dma_start(keepb[k][:, :], keep_d[cols(i, 1), :].to_broadcast([P, G])).then_inc(b_mask[k], 16)
                    for d in range(2):
                        wait(sp, b_ntr, 2 * i + d - 1)
                        sp.dma_start(xn[d][:, :], rows(x1_d, 2 * i + d, XW)).then_inc(b_x[d], 16)
                steps(sp, EG, step)

            @block.vector
            def _(dve):
                def scan_step(i, k, h):
                    wait(dve, b_relu, i + 1)
                    wait(dve, b_mask[k], 16 * h + 16)
                    wait(dve, b_gw, i - 1)
                    wait(dve, b_scan, i)
                    v.tensor_tensor_scan(
                        scan[k][:, :], keepb[k][:, :], hs[k][:, :],
                        0.0 if isinstance(i, int) and i == 0 else scan[1 - k][:, G - 1:G],
                        ALU.mult, ALU.add).then_inc(b_scan, 1)

                def rows_out(i, k, h):
                    wait(dve, b_gw, i + 1)
                    wait(dve, b_put[k], 64 * h)
                    v.tensor_tensor(gr[k][:, :].rearrange("p (j a) -> p j a", a=AW)[:, :, 0:D],
                                    BG[:, :].rearrange("p (j f) -> p j f", f=D),
                                    dinv_t[:, cols(i, J)].unsqueeze(2).to_broadcast([P, J, D]),
                                    ALU.mult).then_inc(b_gr, 1)

                def step(i, k, h):
                    wait(dve, b_get[k], 64 * h + 64)
                    for j in range(J):
                        row, m = xg[k][:, j * XW:j * XW + D], j * XW + D
                        last = v.tensor_scalar(row, row, xg[k][:, m:m + 1], xg[k][:, m + 1:m + 2],
                                               ALU.subtract, ALU.mult)
                    last.then_inc(b_norm, 1)
                    if not isinstance(i, int) or i:
                        scan_step(*before(i, k, h))
                    for d in range(2):
                        wait(dve, b_x[d], 16 * i + 16)
                        x1 = xn[d][:, :].rearrange("p (j a) -> p j a", a=XW)
                        v.tensor_tensor(rs[d][:, 0:J], x1[:, :, D + 1], dinv_n[:, cols(2 * i + d, J)],
                                        ALU.mult).then_inc(b_sc, 1)
                        wait(dve, b_sc, 2 * i + d + 1)
                        for j in range(J):
                            last = v.tensor_scalar(x1[:, j, 0:D], x1[:, j, 0:D], x1[:, j, D:D + 1],
                                                   rs[d][:, j:j + 1], ALU.subtract, ALU.mult)
                        last.then_inc(b_nnorm, 1)
                    if not isinstance(i, int) or i:
                        rows_out(*before(i, k, h))
                steps(dve, EG, step)
                scan_step(EG - 1, (EG - 1) % 2, (EG - 1) // 2)
                rows_out(EG - 1, (EG - 1) % 2, (EG - 1) // 2)

            @block.scalar
            def _(act):
                s = nc.scalar

                def node_relu(i, d):
                    wait(act, b_ntr, 2 * i + d + 1)
                    wait(act, b_nz, 2 * i + d - 1)
                    s.activation(hn[d][:, :], BD[:, :], ACT.Relu).then_inc(b_nrelu, 1)

                def node_out(i, d):
                    wait(act, b_nz, 2 * i + d + 1)
                    wait(act, b_z[d], 16 * i)
                    s.activation(zn[d][:, :], BN[:, :], ACT.Identity, bias=biasc[:, :]).then_inc(b_nzs, 1)
                    wait(act, b_nzs, 2 * i + d + 1)
                    act.dma_start(block_rows(pre_d, 2 * i + d), zn[d][:, :]).then_inc(b_z[d], 16)

                def step(i, k, h):
                    wait(act, b_tr, i + 1)
                    wait(act, b_scan, i - 1)
                    s.activation(hs[k][:, :], T0[:, :], ACT.Relu).then_inc(b_relu, 1)
                    for d in range(2):
                        node_relu(i, d)
                        node_out(i, d)
                steps(act, EG, step)
                for d in range(2):
                    act.wait_ge(b_z[d], 16 * EG)

            @block.tensor
            def _(pe):
                mm = nc.tensor.matmul

                def times_w(i, k, h):
                    wait(pe, b_scan, i + 1)
                    wait(pe, b_gr, i)
                    for j in range(J):
                        last = mm(BG[:, j * D:(j + 1) * D], scan[k][:, j * P:(j + 1) * P], wg[:, :],
                                  start=True, stop=True)
                    last.then_inc(b_gw, 1)

                def step(i, k, h):
                    wait(pe, b_norm, i + 1)
                    wait(pe, b_relu, i)
                    for j in range(J):
                        last = nc.tensor.transpose(T0[:, j * P:(j + 1) * P], xg[k][:, j * XW:j * XW + D], ident[:, :])
                    last.then_inc(b_tr, 1)
                    if not isinstance(i, int) or i:
                        times_w(*before(i, k, h))
                    for d in range(2):
                        wait(pe, b_nnorm, 2 * i + d + 1)
                        wait(pe, b_nrelu, 2 * i + d)
                        for j in range(J):
                            last = nc.tensor.transpose(BD[:, j * P:(j + 1) * P], xn[d][:, j * XW:j * XW + D],
                                                       ident[:, :])
                        last.then_inc(b_ntr, 1)
                        wait(pe, b_nrelu, 2 * i + d + 1)
                        wait(pe, b_nzs, 2 * i + d)
                        mm(BN[:, :], wg[:, :], hn[d][:, :], start=True, stop=True).then_inc(b_nz, 1)
                steps(pe, EG, step)
                times_w(EG - 1, (EG - 1) % 2, (EG - 1) // 2)

        l_ld, l_st = sems("l_ld"), sems("l_st")
        l_sum, l_slope, l_act, l_stats = sem("l_sum"), sem("l_slope"), sem("l_act"), sem("l_stats")

        with nc.Block() as block:
            @block.sync
            def _(sp):
                def step(t, k, h):
                    wait(sp, l_sum, t - 1)
                    sp.dma_start(gn[k][:, :], rows(agg_d, t, AW)).then_inc(l_ld[k], 16)
                    sp.dma_start(hn[k][:, :], block_rows(pre_d, t)).then_inc(l_ld[k], 16)
                steps(sp, NG, step)

            @block.tensor
            def _(pe):
                mm = nc.tensor.matmul

                def step(t, k, h):
                    wait(pe, l_ld[k], 32 * h + 32)
                    wait(pe, l_act, t - 1)
                    mm(BA[k][:, :], ident[:, :], hn[k][:, :], start=True, stop=False)
                    for j in range(J):
                        last = mm(BA[k][:, j * P:(j + 1) * P], gn[k][:, j * AW:j * AW + D], ident[:, :],
                                  start=False, stop=j == J - 1)
                    last.then_inc(l_sum, 1)
                steps(pe, NG, step)

            @block.vector
            def _(dve):
                def step(t, k, h):
                    wait(dve, l_slope, t + 1)
                    wait(dve, l_st[k], 16 * h)
                    v.tensor_tensor(zn[k][:, :], BA[k][:, :], hs[k][:, :], ALU.max).then_inc(l_act, 1)
                    wait(dve, l_act, t + 1)
                    part = zn[k][:, :]
                    if isinstance(t, int) and t == NG - 1:
                        part = part.rearrange("p (j q) -> p j q", j=J)[:, :, DOUBLE:P]
                    v.bn_stats(stats_n[:, t, :] if isinstance(t, int) else stats_n[:, bass.ds(t, 1), :],
                               part).then_inc(l_stats, 1)
                steps(dve, NG, step)

            @block.scalar
            def _(act):
                def store(t, k, h):
                    wait(act, l_act, t + 1)
                    act.dma_start(block_rows(act_d, t), zn[k][:, :]).then_inc(l_st[k], 16)

                def step(t, k, h):
                    wait(act, l_sum, t + 1)
                    wait(act, l_act, t - 1)
                    nc.scalar.activation(hs[k][:, :], BA[k][:, :], ACT.Copy, scale=SLOPE).then_inc(l_slope, 1)
                    if not isinstance(t, int) or t:
                        store(*before(t, k, h))
                steps(act, NG, step)
                store(NG - 1, (NG - 1) % 2, (NG - 1) // 2)
                for k in range(2):
                    act.wait_ge(l_st[k], 16 * (NG // 2))

        o_chain, o_std, o_coef = sem("o_chain"), sem("o_std"), sem("o_coef")
        o_ld, o_st = sems("o_ld"), sems("o_st")
        o_y, o_tr, o_sum = sem("o_y"), sem("o_tr"), sem("o_sum")
        moments, std_c, inv_c, scale_c, shift_c, prod_c = (
            sb(n, [P, w_]) for n, w_ in (("moments", 2), ("std_c", 1), ("inv_c", 1), ("scale_c", 1),
                                         ("shift_c", 1), ("prod_c", 1)))

        with nc.Block() as block:
            @block.sync
            def _(sp):
                def step(t, k, h):
                    wait(sp, o_y, t - 1)
                    sp.dma_start(hn[k][:, :], block_rows(act_d, t)).then_inc(o_ld[k], 16)
                    wait(sp, o_sum, t - 1)
                    sp.dma_start(xn[k][:, :], rows(x1_d, t, XW)).then_inc(o_ld[k], 16)
                steps(sp, NG, step)

            @block.vector
            def _(dve):
                v.bn_aggr(moments[:, :], stats_n[:, :, :].rearrange("p t s -> p (t s)")).then_inc(o_chain, 1)
                dve.wait_ge(o_std, 1)
                v.reciprocal(inv_c[:, :], std_c[:, :]).then_inc(o_chain, 1)
                dve.wait_ge(o_chain, 2)
                v.tensor_tensor(scale_c[:, :], gammac[:, :], inv_c[:, :], ALU.mult).then_inc(o_chain, 1)
                dve.wait_ge(o_chain, 3)
                v.tensor_tensor(prod_c[:, :], moments[:, 0:1], scale_c[:, :], ALU.mult).then_inc(o_chain, 1)
                dve.wait_ge(o_chain, 4)
                v.tensor_tensor(shift_c[:, :], betac[:, :], prod_c[:, :], ALU.subtract).then_inc(o_coef, 1)

                def step(t, k, h):
                    wait(dve, o_tr, t + 1)
                    wait(dve, o_ld[k], 32 * h + 32)
                    wait(dve, o_st[k], 16 * h)
                    v.tensor_tensor(xc[k][:, :].rearrange("p (j f) -> p j f", f=D),
                                    BX[k][:, :].rearrange("p (j f) -> p j f", f=D),
                                    xn[k][:, :].rearrange("p (j a) -> p j a", a=XW)[:, :, 0:D],
                                    ALU.add).then_inc(o_sum, 1)
                steps(dve, NG, step)

            @block.scalar
            def _(act):
                s = nc.scalar
                act.wait_ge(o_chain, 1)
                s.activation(std_c[:, :], moments[:, 1:2], ACT.Sqrt, bias=eps_col[:, :]).then_inc(o_std, 1)
                act.wait_ge(o_coef, 1)

                def store(t, k, h):
                    wait(act, o_sum, t + 1)
                    if isinstance(t, int) and t == NG - 1:
                        act.wait_ge(o_st[1 - k], 16 * (NG // 2))
                    act.dma_start(rows(out, t, D), xc[k][:, :]).then_inc(o_st[k], 16)

                def step(t, k, h):
                    wait(act, o_ld[k], 32 * h + 32)
                    wait(act, o_tr, t - 1)
                    s.activation(zn[k][:, :], hn[k][:, :], ACT.Identity, bias=shift_c[:, :],
                                 scale=scale_c[:, :]).then_inc(o_y, 1)
                    if not isinstance(t, int) or t:
                        store(*before(t, k, h))
                steps(act, NG, step)
                store(NG - 1, (NG - 1) % 2, (NG - 1) // 2)
                for k in range(2):
                    act.wait_ge(o_st[k], 16 * (NG // 2))

            @block.tensor
            def _(pe):
                def step(t, k, h):
                    wait(pe, o_y, t + 1)
                    wait(pe, o_sum, t - 1)
                    for j in range(J):
                        last = nc.tensor.transpose(BX[k][:, j * D:(j + 1) * D], zn[k][:, j * P:(j + 1) * P],
                                                   ident[:, :])
                    last.then_inc(o_tr, 1)
                steps(pe, NG, step)


_INPUTS = ["x", "src", "dst", "edge_weight", "L0_gnn_W1", "L0_gnn_b1", "L0_gnn_W2", "L0_gnn_b2", "L0_gnn_U1",
           "L0_gnn_c1", "L0_gnn_U2", "L0_gnn_c2", "L1_gnn_W", "L1_gnn_bias", "L1_gnn_gamma", "L1_gnn_beta"]


def kernel(**inputs):
    import numpy as np
    import concourse.bacc as bacc
    from concourse import mybir as mb
    from concourse.bass_utils import run_bass_kernel_spmd

    nc = bacc.Bacc("TRN2", target_bir_lowering=False, num_devices=1)
    arrays, args = {}, []
    for name in _INPUTS:
        a = np.ascontiguousarray(inputs[name])
        arrays[f"in_{name}"] = a
        args.append(nc.dram_tensor(f"in_{name}", a.shape, mb.dt.from_np(a.dtype), kind="ExternalInput").ap())
    out = nc.dram_tensor("out_x", arrays["in_x"].shape, mb.dt.float32, kind="ExternalOutput").ap()
    gnn_kernel(nc, *args, out)
    r = run_bass_kernel_spmd(nc, [arrays], core_ids=[0])
    return r.results[0]["out_x"]
```

```python
from contextlib import ExitStack

import concourse.bass as bass
from concourse import mybir

F32 = mybir.dt.float32
BF16 = mybir.dt.bfloat16
I32 = mybir.dt.int32
ALU = mybir.AluOpType
ACT = mybir.ActivationFunctionType

P = 128
D = 128
J = 4
G = P * J
LN_EPS = 1e-5
BN_EPS = 1e-5
SLOPE = 0.01
XW = D + 3
MEAN, SCALE, DINV = D, D + 1, D + 2
RESTART = 1e30


def gnn_kernel(nc, x, src, dst, w, W1, b1, W2, b2, U1, c1, U2, c2, W, bias, gamma, beta, out):
    N = x.shape[0]
    E = src.shape[0]
    EG = -(-E // G)
    ET = EG * J
    NG = -(-N // G)
    LAST_BASE = N - G
    DOUBLE = ((NG - 1) * G - LAST_BASE) // J
    assert NG == 2 * EG and EG % 2 == 1 and ((NG - 1) * G - LAST_BASE) % J == 0
    EC = 2 * P
    EQ = EG * G // EC
    EFULL = E // EC
    EREST = E - EFULL * EC
    assert EQ == EFULL + 1 and EREST > 1
    NOWHERE = 2 * N
    x1_d = nc.dram_tensor("x1_d", (N, XW), F32, kind="Internal").ap()
    xe_d = nc.dram_tensor("xe_d", (EG * P, J * XW), F32, kind="Internal").ap()
    act_d = nc.dram_tensor("act_d", (NG * P, G), F32, kind="Internal").ap()
    acte_d = nc.dram_tensor("acte_d", (EG * P, G), F32, kind="Internal").ap()
    pen_d = nc.dram_tensor("pen_d", (EG, G), F32, kind="Internal").ap()
    keep_d = nc.dram_tensor("keep_d", (EG, G), F32, kind="Internal").ap()
    share_d = nc.dram_tensor("share_d", (EG, G), F32, kind="Internal").ap()
    w_d = nc.dram_tensor("w_d", (EQ, 9, EC), BF16, kind="Internal").ap()

    def rows(table, t, width):
        if isinstance(t, int):
            base = min(t * G, LAST_BASE)
            part = table[base:base + G, 0:width]
        else:
            part = table[bass.ds(t * G, G), 0:width]
        return part.rearrange("(p j) f -> p (j f)", j=J)

    def block_rows(table, t):
        return table[bass.ds(t * P, P), :] if not isinstance(t, int) else table[t * P:(t + 1) * P, :]

    def cols(t, n):
        return bass.ds(t * n, n) if not isinstance(t, int) else slice(t * n, (t + 1) * n)

    ctx = ExitStack()
    with ctx:
        def sb(name, shape, dt=F32):
            return ctx.enter_context(nc.sbuf_tensor(name, shape, dt))

        def sem(name):
            return ctx.enter_context(nc.semaphore(name))

        def sems(name, n=2):
            return [sem(f"{name}{k}") for k in range(n)]

        ident = sb("ident", [P, P])
        ones_row = sb("ones_row", [1, P])
        w1a, w1b, w2 = sb("w1a", [P, D]), sb("w1b", [P, D]), sb("w2", [P, D])
        u1a, u1b, u2, wg = sb("u1a", [P, D]), sb("u1b", [P, D]), sb("u2", [P, D]), sb("wg", [P, D])
        w1w = sb("w1w", [1, D])
        w1w_parts = [sb(f"w1w_part{n}", [1, D], BF16) for n in range(3)]
        w1w9 = sb("w1w9", [9, D], BF16)
        b1c, b2c, c1c, biasc = sb("b1c", [P, 1]), sb("b2c", [P, 1]), sb("c1c", [P, 1]), sb("biasc", [P, 1])
        gammac, betac = sb("gammac", [P, 1]), sb("betac", [P, 1])
        eps_col, one_col = sb("eps_col", [P, 1]), sb("one_col", [P, 1])
        c2_row = sb("c2_row", [1, G])
        c2_parts = [sb(f"c2_part{n}", [1, G], BF16) for n in range(3)]
        c2_three = sb("c2_three", [3, G], BF16)
        ones_bf = sb("ones_bf", [3, P], BF16)
        src_t, dst_t, put_t = sb("src_t", [P, ET], I32), sb("dst_t", [P, ET], I32), sb("put_t", [P, ET], I32)
        late_t = sb("late_t", [P, ET], I32)
        count_t, dinv_t = sb("count_t", [P, ET]), sb("dinv_t", [P, ET])
        stats = sb("stats", [P, NG + EG, 6])

        def ring(name, shape, n=2, dt=F32):
            return [sb(f"{name}{k}", shape, dt) for k in range(n)]

        xg = ring("xg", [P, 2 * J * XW], 4)
        hg = ring("hg", [P, G])
        hs, hd = ring("hs", [P, G]), ring("hd", [P, G], 4)
        ze, ms = ring("ze", [P, G]), ring("ms", [P, G])
        scan = ring("scan", [P, G])
        keepb = ring("keepb", [P, G], 4)
        wrow = ring("wrow", [9, G], 2, BF16)
        zr = ring("zr", [P, G])
        xe = ring("xe", [P, J * XW], 4)
        get_idx = ring("get_idx", [P, 2 * J], 4, I32)
        put_idx = ring("put_idx", [P, J], 4, I32)
        xn = ring("xn", [P, G], 8)
        hn = ring("hn", [P, G], 4)
        tn = ring("tn", [P, G])
        zn = ring("zn", [P, G], 4)
        x1n = ring("x1n", [P, J * XW], 4)
        st0, mv0, sd0, rs0 = (ring(n, [P, 16] + w_) for n, w_ in (("st0", [6]), ("mv0", [2]), ("sd0", []), ("rs0", [])))
        nb0 = ring("nb0", [P, 3 * J])
        st1, sd1, rs1 = (ring(n, [P, 12] + w_) for n, w_ in (("st1", [6]), ("sd1", []), ("rs1", [])))

        bank = [ctx.enter_context(nc.psum_tensor(f"bank{k}", [P, 512], F32)) for k in range(8)]

        dst_a, prev_a, next_a, src_a = (sb(n, [P, EC], I32) for n in ("dst_a", "prev_a", "next_a", "src_a"))
        w_a = sb("w_a", [P, EC])
        pen_a, keep_a, local_a, allkeep_a, count_a, put_a = (
            sb(n, [P, EC]) for n in ("pen_a", "keep_a", "local_a", "allkeep_a", "count_a", "put_a"))
        srcf_a, dstf_a, same_a = sb("srcf_a", [P, EC]), sb("dstf_a", [P, EC]), sb("same_a", [P, EC])
        ones_a, zeros_a = sb("ones_a", [P, EC]), sb("zeros_a", [P, EC])
        ends_r = sb("ends_r", [1, 2 * EQ])
        carry_r = sb("carry_r", [1, EQ + 1])
        carry_c = sb("carry_c", [P, 1])
        share_a, deg_a = sb("share_a", [P, EC]), sb("deg_a", [P, EC])
        rest_row = ring("rest_row", [1, G])
        rest_a = ring("rest_a", [P, EC])
        w_parts = ring("w_part", [P, EC], 3, BF16)

        s_blank = sem("s_blank")
        s_fill = sem("s_fill")
        s_weights = sem("s_weights")
        s_edges = sem("s_edges")
        bound_i, bound_f = sb("bound_i", [P, 1], I32), sb("bound_f", [P, 1])
        above_a, late_a, now_a = (sb(n, [P, EC]) for n in ("above_a", "late_a", "now_a"))
        s_bound = sem("s_bound")
        s_late = sem("s_late")
        islate_a = sb("islate_a", [P, EC])
        lates_r, upto_r = sb("lates_r", [1, EC]), sb("upto_r", [1, EC])
        any_late = sb("any_late", [1, 1], I32)
        s_flag = sem("s_flag")
        s_split = sem("s_split")
        s_deg = sem("s_deg")
        s_id = sem("s_id")
        s_arr = sem("s_arr")
        s_ends = sem("s_ends")
        s_carry = sem("s_carry")
        s_tr = sem("s_tr")
        s_tv = sem("s_tv")
        s_dv = sem("s_dv")
        s_masks = sem("s_masks")

        def col(v):
            return v.rearrange("(p o) -> p o", o=1)

        weight_loads = [
            (w1a[:, :], W1[0:D, :]), (w1b[:, :], W1[D:2 * D, :]), (w1w[:, :], W1[2 * D:2 * D + 1, :]),
            (w2[:, :], W2[:, :]), (u1a[:, :], U1[0:D, :]), (u1b[:, :], U1[D:2 * D, :]),
            (u2[:, :], U2[:, :]), (wg[:, :], W[:, :]),
            (b1c[:, :], col(b1)), (b2c[:, :], col(b2)), (c1c[:, :], col(c1)), (biasc[:, :], col(bias)),
            (gammac[:, :], col(gamma)), (betac[:, :], col(beta)),
        ] + [(c2_row[:, j * D:(j + 1) * D], c2.rearrange("(o f) -> o f", o=1)) for j in range(J)]
        N_WEIGHTS = len(weight_loads)

        with nc.Block() as block:
            @block.gpsimd
            def _(g):
                g.memset(dst_a[:, :], N).then_inc(s_blank, 1)
                g.memset(prev_a[:, :], -1).then_inc(s_blank, 1)
                g.memset(next_a[:, :], N).then_inc(s_blank, 1)
                g.memset(src_a[:, :], 0).then_inc(s_blank, 1)
                g.memset(w_a[:, :], 0.0).then_inc(s_blank, 1)
                g.iota(bound_i[:, :], pattern=[[0, 1]], base=G, channel_multiplier=G).then_inc(s_bound, 1)
                g.memset(ident[:, :], 0.0).then_inc(s_id, 1)
                g.wait_ge(s_id, 1)
                g.affine_select(out=ident[:, :], in_=ident[:, :], compare_op=ALU.not_equal, fill=1.0,
                                base=0, pattern=[[-1, P]], channel_multiplier=1).then_inc(s_id, 1)

            @block.sync
            def _(sp):
                def flat(v, a, b):
                    return v[a:b].rearrange("(q c) -> q c", c=EC)

                def line(v, a, b):
                    return v[a:b].rearrange("(q c) -> q c", q=1)

                sp.wait_ge(s_blank, 5)
                full = EFULL * EC
                for tile, v in ((dst_a, dst), (src_a, src), (w_a, w)):
                    sp.dma_start(tile[0:EFULL, :], flat(v, 0, full)).then_inc(s_edges, 16)
                    sp.dma_start(tile[EFULL:EQ, 0:EREST], line(v, full, E)).then_inc(s_edges, 16)
                sp.dma_start(prev_a[0:1, 1:EC], line(dst, 0, EC - 1)).then_inc(s_edges, 16)
                sp.dma_start(prev_a[1:EFULL, :], flat(dst, EC - 1, full - 1)).then_inc(s_edges, 16)
                sp.dma_start(prev_a[EFULL:EQ, 0:EREST], line(dst, full - 1, E - 1)).then_inc(s_edges, 16)
                sp.dma_start(next_a[0:EFULL, :], flat(dst, 1, full + 1)).then_inc(s_edges, 16)
                sp.dma_start(next_a[EFULL:EQ, 0:EREST - 1], line(dst, full + 1, E)).then_inc(s_edges, 16)
                sp.wait_ge(s_edges, 16 * 11)
                sp.wait_ge(s_arr, 2)
                sp.dma_start(pen_d.rearrange("s (h c) -> (s h) c", c=EC), pen_a[0:EQ, :]).then_inc(s_masks, 16)
                sp.dma_start(keep_d.rearrange("s (h c) -> (s h) c", c=EC), keep_a[0:EQ, :]).then_inc(s_masks, 16)
                sp.wait_ge(s_dv, 6)
                sp.dma_start(share_d.rearrange("s (h c) -> (s h) c", c=EC), share_a[0:EQ, :]).then_inc(s_masks, 16)
                sp.wait_ge(s_weights, 16 * N_WEIGHTS)

            @block.scalar
            def _(act):
                for to, of in weight_loads:
                    act.dma_start(to, of).then_inc(s_weights, 16)
                act.wait_ge(s_arr, 12)
                nc.scalar.activation(deg_a[0:EQ, :], count_a[0:EQ, :], ACT.Sqrt, bias=one_col[0:EQ, :]).then_inc(s_deg, 1)
                act.wait_ge(s_tv, 5)
                nc.scalar.activation(dinv_t[:, :], count_t[:, :], ACT.Sqrt, bias=one_col[:, :]).then_inc(s_deg, 1)

            @block.vector
            def _(dve):
                v = nc.vector
                v.memset(ones_a[:, :], 1.0).then_inc(s_fill, 1)
                v.memset(zeros_a[:, :], 0.0).then_inc(s_fill, 1)
                v.memset(eps_col[:, :], LN_EPS).then_inc(s_fill, 1)
                v.memset(one_col[:, :], 1.0).then_inc(s_fill, 1)
                v.memset(ones_row[:, :], 1.0).then_inc(s_fill, 1)
                v.memset(carry_r[:, :], 0.0).then_inc(s_fill, 1)
                dve.wait_ge(s_edges, 16 * 11)
                dve.wait_ge(s_fill, 6)
                q = slice(0, EQ)
                v.tensor_tensor(same_a[q, :], prev_a[q, :], dst_a[q, :], ALU.subtract).then_inc(s_dv, 1)
                dve.wait_ge(s_dv, 1)
                v.tensor_scalar(pen_a[q, :], same_a[q, :], RESTART, None, ALU.mult).then_inc(s_arr, 1)
                v.tensor_scalar(keep_a[q, :], same_a[q, :], 0.0, None, ALU.is_equal).then_inc(s_arr, 1)
                dve.wait_ge(s_arr, 2)
                v.tensor_tensor_scan(local_a[q, :], keep_a[q, :], ones_a[q, :], 0.0, ALU.mult, ALU.add).then_inc(s_arr, 1)
                v.tensor_tensor_scan(allkeep_a[q, :], keep_a[q, :], zeros_a[q, :], 1.0, ALU.mult, ALU.add).then_inc(s_arr, 1)
                v.tensor_copy(srcf_a[q, :], src_a[q, :]).then_inc(s_arr, 1)
                v.tensor_copy(dstf_a[q, :], dst_a[q, :]).then_inc(s_arr, 1)
                v.tensor_copy(count_a[q, :], next_a[q, :]).then_inc(s_arr, 1)
                dve.wait_ge(s_arr, 7)
                v.tensor_tensor(same_a[q, :], count_a[q, :], dstf_a[q, :], ALU.is_equal).then_inc(s_arr, 1)
                dve.wait_ge(s_arr, 8)
                v.scalar_tensor_tensor(out=put_a[q, :], in0=same_a[q, :], scalar=float(NOWHERE), in1=dstf_a[q, :],
                                       op0=ALU.mult, op1=ALU.add).then_inc(s_arr, 1)
                dve.wait_ge(s_bound, 1)
                v.tensor_copy(bound_f[:, :], bound_i[:, :]).then_inc(s_late, 1)
                dve.wait_ge(s_late, 1)
                v.tensor_scalar(above_a[q, :], dstf_a[q, :], bound_f[q, :], float(NOWHERE),
                                ALU.is_ge, ALU.mult).then_inc(s_late, 1)
                dve.wait_ge(s_late, 2)
                dve.wait_ge(s_arr, 9)
                v.scalar_tensor_tensor(out=late_a[q, :], in0=put_a[q, :], scalar=float(NOWHERE), in1=above_a[q, :],
                                       op0=ALU.add, op1=ALU.subtract).then_inc(s_late, 1)
                v.tensor_tensor(now_a[q, :], put_a[q, :], above_a[q, :], ALU.add).then_inc(s_late, 1)
                dve.wait_ge(s_late, 4)
                v.tensor_scalar(islate_a[q, :], late_a[q, :], float(N), None, ALU.is_lt).then_inc(s_late, 1)
                dve.wait_ge(s_ends, 1)
                v.tensor_copy(ends_r[:, :], bank[0][0:1, 0:2 * EQ]).then_inc(s_arr, 1)
                dve.wait_ge(s_arr, 10)
                v.tensor_tensor_scan(carry_r[:, 1:EQ + 1], ends_r[:, EQ:2 * EQ], ends_r[:, 0:EQ], 0.0,
                                     ALU.mult, ALU.add).then_inc(s_arr, 1)
                dve.wait_ge(s_carry, 1)
                v.tensor_copy(carry_c[q, :], bank[1][q, 0:1]).then_inc(s_dv, 1)
                dve.wait_ge(s_dv, 2)
                v.scalar_tensor_tensor(out=count_a[q, :], in0=allkeep_a[q, :], scalar=carry_c[q, :], in1=local_a[q, :],
                                       op0=ALU.mult, op1=ALU.add).then_inc(s_arr, 1)
                for k, to in enumerate((src_t, dst_t, put_t, late_t, count_t)):
                    dve.wait_ge(s_tr, k + 1)
                    v.tensor_copy(to[:, :].rearrange("p (q h) -> p h q", h=2),
                                  bank[2 + k][:, 0:2 * EQ].rearrange("p (h q) -> p h q", h=2)).then_inc(s_tv, 1)
                dve.wait_ge(s_flag, 1)
                v.tensor_copy(lates_r[:, :], bank[7][0:1, 0:EC]).then_inc(s_flag, 1)
                dve.wait_ge(s_flag, 2)
                v.tensor_tensor_scan(upto_r[:, :], ones_a[0:1, :], lates_r[:, :], 0.0, ALU.mult, ALU.add).then_inc(s_flag, 1)
                dve.wait_ge(s_flag, 3)
                v.tensor_copy(any_late[:, :], upto_r[:, EC - 1:EC]).then_inc(s_flag, 1)
                dve.wait_ge(s_deg, 2)
                v.reciprocal(dinv_t[:, :], dinv_t[:, :]).then_inc(s_dv, 1)
                v.reciprocal(share_a[q, :], deg_a[q, :]).then_inc(s_dv, 1)
                dve.wait_ge(s_dv, 4)
                v.tensor_tensor(deg_a[q, :], share_a[q, :], same_a[q, :], ALU.mult).then_inc(s_dv, 1)
                dve.wait_ge(s_dv, 5)
                v.tensor_tensor(share_a[q, :], share_a[q, :], deg_a[q, :], ALU.subtract).then_inc(s_dv, 1)
                for tile in x1n:
                    v.memset(tile[:, :], 1.0).then_inc(s_fill, 1)

            @block.tensor
            def _(pe):
                pe.wait_ge(s_id, 2)
                pe.wait_ge(s_arr, 4)
                for k, of in enumerate((local_a, allkeep_a)):
                    last = nc.tensor.matmul(bank[0][0:1, k * EQ:(k + 1) * EQ], of[0:EQ, EC - 1:EC],
                                            ident[0:EQ, 0:EQ], start=True, stop=True)
                last.then_inc(s_ends, 1)
                pe.wait_ge(s_arr, 11)
                nc.tensor.matmul(bank[1][0:EQ, 0:1], carry_r[:, 0:EQ], ones_row[:, 0:1],
                                 start=True, stop=True).then_inc(s_carry, 1)
                for k, of in enumerate((srcf_a, dstf_a, now_a, late_a, count_a)):
                    if k == 2:
                        pe.wait_ge(s_late, 4)
                    if k == 4:
                        pe.wait_ge(s_arr, 12)
                        pe.wait_ge(s_late, 5)
                        nc.tensor.matmul(bank[7][0:1, 0:EC], one_col[0:EQ, :], islate_a[0:EQ, :],
                                         start=True, stop=True).then_inc(s_flag, 1)
                    for h in range(2):
                        last = nc.tensor.transpose(bank[2 + k][:, h * EQ:(h + 1) * EQ],
                                                   of[0:EQ, h * P:(h + 1) * P], ident[0:EQ, 0:EQ])
                    last.then_inc(s_tr, 1)

        def wait(eng, signal, value):
            if not isinstance(value, int) or value > 0:
                eng.wait_ge(signal, value)

        def hold(eng, signal, value):
            if not isinstance(value, int) or value > 0:
                eng.wait_ge(signal, value)
                eng.sem_inc(s_held, 1)

        def steps(eng, n, step):
            for i in range(8):
                step(i, i % 4, i // 4)
            with eng.Fori(2, (n - 1) // 4) as h:
                for k in range(4):
                    step(4 * h + k, k, h)
            for i in range((n - 1) // 4 * 4, n):
                step(i, i % 4, i // 4)

        def back(n, i, k, h):
            return i - n, (k - n) % 4, h + (k - n) // 4

        def there(i):
            return not isinstance(i, int) or 0 <= i < EG

        def fill2(k, h):
            return 2 * h + k // 2

        def by_tile(tile, width):
            return tile[:, :].rearrange("p (j a) -> p j a", a=width)

        s_held = sem("s_held")

        def late_rows(g, table, of, width, landing, signal, indexed):
            g.wait_ge(s_flag, 4)
            late = g.value_load(any_late[0:1, 0:1])
            with g.If(late > 0):
                with g.Fori(0, EG) as i:
                    g.dma_start(landing[:, :], block_rows(of, i)).then_inc(signal, 16)
                    g.tensor_copy(put_idx[0][:, :], late_t[:, cols(i, J)]).then_inc(indexed, 1)
                    hold(g, signal, 80 * i + 16)
                    hold(g, indexed, EG + i + 1)
                    for j in range(J):
                        g.indirect_dma_start(
                            out=table[:, :], in_=landing[:, j * width:(j + 1) * width],
                            out_offset=bass.IndirectOffsetOnAxis(ap=put_idx[0][:, j:j + 1], axis=0),
                            in_offset=None, bounds_check=N - 1, oob_is_err=False).then_inc(signal, 16)
                    hold(g, signal, 80 * i + 80)
        v, s, mm, tr = nc.vector, nc.scalar, nc.tensor.matmul, nc.tensor.transpose

        a_get = sems("a_get", 4)
        a_mask = sems("a_mask", 4)
        a_w = sems("a_w")
        a_put = sems("a_put", 4)
        a_lin = sems("a_lin", 4)
        a_x = sems("a_x", 8)
        a_x1 = sems("a_x1", 4)
        a_late = sem("a_late")
        a_gi, a_pi = sem("a_gi"), sem("a_pi")
        a_st, a_mv, a_sd, a_rs, a_nb = (sem("a_" + n) for n in ("st", "mv", "sd", "rs", "nb"))
        a_norm, a_dnorm = sem("a_norm"), sem("a_dnorm")
        a_tr = sem("a_tr")
        a_relu = sem("a_relu")
        a_hid = sem("a_hid")
        a_ze = sem("a_ze")
        a_msg = sem("a_msg")
        a_ms = sem("a_ms")
        a_scan = sem("a_scan")
        a_pre = sem("a_pre")
        a_zr = sem("a_zr")
        a_nnorm, a_ntr, a_ntn, a_npre, a_nzn = (sem("a_" + n) for n in ("nnorm", "ntr", "ntn", "npre", "nzn"))
        a_ue, a_un = sem("a_ue"), sem("a_un")
        a_ge, a_ne = sem("a_ge"), sem("a_ne")
        a_st1, a_mv1, a_sd1, a_rs1 = (sem("a_" + n) for n in ("st1", "mv1", "sd1", "rs1"))
        a_fe, a_fn = sem("a_fe"), sem("a_fn")
        BT, BZ, BM, BN, BX = bank[0:2], bank[2], bank[3], bank[4], bank[5:8]

        with nc.Block() as block:
            @block.gpsimd
            def _(g):
                def gather(i, k, h):
                    hold(g, a_tr, i - 3)
                    hold(g, a_ge, i - 3)
                    g.tensor_copy(get_idx[k][:, 0:J], src_t[:, cols(i, J)]).then_inc(a_gi, 1)
                    g.tensor_copy(get_idx[k][:, J:2 * J], dst_t[:, cols(i, J)]).then_inc(a_gi, 1)
                    hold(g, a_gi, 2 * i + 2)
                    for j in range(2 * J):
                        g.indirect_dma_start(
                            out=xg[k][:, j * D:(j + 1) * D], out_offset=None, in_=x[:, :],
                            in_offset=bass.IndirectOffsetOnAxis(ap=get_idx[k][:, j:j + 1], axis=0),
                            bounds_check=N - 1, oob_is_err=False).then_inc(a_get[k], 16)

                def scatter(i, k, h):
                    hold(g, a_put[k], 64 * h)
                    g.tensor_copy(put_idx[k][:, :], put_t[:, cols(i, J)]).then_inc(a_pi, 1)
                    hold(g, a_pi, i + 1)
                    hold(g, a_fe, i + 1)
                    for d in range(2):
                        hold(g, a_x1[2 * (k % 2) + d], 16 * fill2(k, h) + 16)
                        wait_prev = 16 * (fill2(k, h) + (k % 2))
                        hold(g, a_x1[2 * (1 - k % 2) + d], wait_prev)
                    for j in range(J):
                        g.indirect_dma_start(
                            out=x1_d[:, :], in_=xe[k][:, j * XW:(j + 1) * XW],
                            out_offset=bass.IndirectOffsetOnAxis(ap=put_idx[k][:, j:j + 1], axis=0),
                            in_offset=None, bounds_check=N - 1, oob_is_err=False).then_inc(a_put[k], 16)

                def step(i, k, h):
                    gather(i, k, h)
                    if there(back(6, i, k, h)[0]):
                        scatter(*back(6, i, k, h))
                steps(g, EG, step)
                for i in range(EG - 6, EG):
                    scatter(i, i % 4, i // 4)
                for k in range(4):
                    g.wait_ge(a_put[k], 64 * ((EG + 3 - k) // 4))
                    g.wait_ge(a_lin[k], 16 * ((EG + 3 - k) // 4))
                    g.wait_ge(a_x1[k], 16 * ((EG + 1 - k // 2) // 2))
                late_rows(g, x1_d, xe_d, XW, xe[0], a_late, a_pi)

            @block.sync
            def _(sp):
                def step(i, k, h):
                    for d in range(2):
                        wait(sp, a_ne, 2 * (i - 4) + d + 1)
                        sp.dma_start(xn[2 * k + d][:, :], rows(x, 2 * i + d, D)).then_inc(a_x[2 * k + d], 16)
                    k2 = k % 2
                    wait(sp, a_scan, i - 3)
                    sp.dma_start(keepb[k][:, :], pen_d[cols(i, 1), :].to_broadcast([P, G])).then_inc(a_mask[k], 16)
                    wait(sp, a_hid, i - 1)
                    sp.dma_start(wrow[k2][:, :], w_d[cols(i, 2), :, :].rearrange("h r c -> r h c")).then_inc(a_w[k2], 16)
                sp.wait_ge(s_split, 15)
                for n in range(3):
                    sp.dma_start(c2_three[n:n + 1, :], c2_parts[n][:, :]).then_inc(s_masks, 16)
                    for m in range(3):
                        sp.dma_start(w1w9[3 * m + n:3 * m + n + 1, :], w1w_parts[n][:, :]).then_inc(s_masks, 16)
                        sp.dma_start(w_d[:, 3 * n + m, :], w_parts[n][0:EQ, :]).then_inc(s_masks, 16)
                sp.wait_ge(s_masks, 16 * 24)
                steps(sp, EG, step)

            @block.vector
            def _(dve):
                q = slice(0, EQ)

                def finish(i, k, h):
                    k2 = k % 2
                    wait(dve, a_sd1, i + 1)
                    v.reciprocal(rs1[k2][:, :], sd1[k2][:, :]).then_inc(a_rs1, 1)
                    wait(dve, a_rs1, i + 1)
                    edge_rows = by_tile(xe[k], XW)
                    v.tensor_tensor(edge_rows[:, :, SCALE], rs1[k2][:, 0:J], dinv_t[:, cols(i, J)], ALU.mult)
                    v.tensor_copy(edge_rows[:, :, DINV], dinv_t[:, cols(i, J)]).then_inc(a_fe, 1)
                    for d in range(2):
                        v.tensor_copy(by_tile(x1n[2 * k2 + d], XW)[:, :, SCALE],
                                      rs1[k2][:, J + J * d:2 * J + J * d]).then_inc(a_fn, 1)

                def add_edges(i, k, h):
                    wait(dve, a_ue, i + 1)
                    wait(dve, a_put[k], 64 * h)
                    wait(dve, a_lin[k], 16 * h)
                    v.tensor_tensor(by_tile(xe[k], XW)[:, :, 0:D], by_tile(BX[0], D),
                                    xg[k][:, G:2 * G].rearrange("p (j a) -> p j a", a=D),
                                    ALU.add).then_inc(a_ge, 1)

                def add_nodes(i, k, h):
                    for d in range(2):
                        k4 = 2 * (k % 2) + d
                        wait(dve, a_un, 2 * i + d + 1)
                        wait(dve, a_x1[k4], 16 * fill2(k, h))
                        v.tensor_tensor(by_tile(x1n[k4], XW)[:, :, 0:D], by_tile(BX[1 + d], D),
                                        by_tile(xn[2 * k + d], D), ALU.add).then_inc(a_ne, 1)

                def statistics1(i, k, h):
                    k2 = k % 2
                    parts = [by_tile(tile, XW) for tile in (xe[k], x1n[2 * k2], x1n[2 * k2 + 1])]
                    wait(dve, a_ge, i + 1)
                    wait(dve, a_ne, 2 * i + 2)
                    for n, tile in enumerate(parts):
                        for j in range(J):
                            last = v.bn_stats(st1[k2][:, J * n + j, :], tile[:, j, 0:D])
                    last.then_inc(a_st1, 1)
                    hold(dve, a_st1, i + 1)
                    for n, tile in enumerate(parts):
                        for j in range(J):
                            last = v.bn_aggr(tile[:, j, MEAN:MEAN + 2], st1[k2][:, J * n + j, :])
                    last.then_inc(a_mv1, 1)

                def scan_step(i, k, h):
                    wait(dve, a_ms, i + 1)
                    wait(dve, a_mask[k], 16 * h + 16)
                    wait(dve, a_pre, i - 1)
                    wait(dve, a_scan, i)
                    v.tensor_tensor_scan(
                        scan[k % 2][:, :], keepb[k][:, :], ms[k % 2][:, :],
                        -RESTART if isinstance(i, int) and i == 0 else scan[1 - k % 2][:, G - 1:G],
                        ALU.add, ALU.max).then_inc(a_scan, 1)

                def statistics(i, k, h):
                    k2 = k % 2
                    wait(dve, a_get[k], 128 * h + 128)
                    for j in range(2 * J):
                        v.bn_stats(st0[k2][:, j, :], xg[k][:, j * D:(j + 1) * D])
                    for d in range(2):
                        wait(dve, a_x[2 * k + d], 16 * h + 16)
                        for j in range(J):
                            last = v.bn_stats(st0[k2][:, 2 * J + J * d + j, :], xn[2 * k + d][:, j * D:(j + 1) * D])
                    last.then_inc(a_st, 1)

                def moments(i, k, h):
                    hold(dve, a_st, i + 1)
                    for j in range(4 * J):
                        last = v.bn_aggr(mv0[k % 2][:, j, :], st0[k % 2][:, j, :])
                    last.then_inc(a_mv, 1)

                def normalise(i, k, h):
                    k2 = k % 2
                    wait(dve, a_sd, i + 1)
                    v.reciprocal(rs0[k2][:, :], sd0[k2][:, :]).then_inc(a_rs, 1)
                    wait(dve, a_rs, i + 1)
                    wait(dve, a_nnorm, 2 * i - 2)
                    v.scalar_tensor_tensor(out=nb0[k2][:, :], in0=mv0[k2][:, J:4 * J, 0], scalar=-1.0,
                                           in1=rs0[k2][:, J:4 * J], op0=ALU.mult, op1=ALU.mult).then_inc(a_nb, 1)
                    for j in range(J):
                        row = xg[k][:, j * D:(j + 1) * D]
                        last = v.tensor_scalar(row, row, mv0[k2][:, j, 0:1], rs0[k2][:, j:j + 1],
                                               ALU.subtract, ALU.mult)
                    last.then_inc(a_norm, 1)

                def step(i, k, h):
                    if there(i):
                        normalise(i, k, h)
                    if there(back(2, i, k, h)[0]):
                        add_edges(*back(2, i, k, h))
                        add_nodes(*back(2, i, k, h))
                    if there(back(1, i, k, h)[0]):
                        scan_step(*back(1, i, k, h))
                    if there(back(-1, i, k, h)[0]):
                        statistics(*back(-1, i, k, h))
                    if there(back(3, i, k, h)[0]):
                        finish(*back(3, i, k, h))
                    if there(back(-1, i, k, h)[0]):
                        moments(*back(-1, i, k, h))
                    if there(back(2, i, k, h)[0]):
                        statistics1(*back(2, i, k, h))
                v.memset(ones_bf[:, :], 1.0).then_inc(s_fill, 1)
                dve.wait_ge(s_weights, 16 * N_WEIGHTS)
                for n, (of, parts, rest) in enumerate((
                        (c2_row[:, :], [p[:, :] for p in c2_parts], [r[:, :] for r in rest_row]),
                        (w1w[:, :], [p[:, :] for p in w1w_parts], [r[:, 0:D] for r in rest_row]),
                        (w_a[q, :], [p[q, :] for p in w_parts], [r[q, :] for r in rest_a]))):
                    if n > 0:
                        dve.wait_ge(s_split, 5 * n)
                    v.tensor_copy(parts[0], of).then_inc(s_split, 1)
                    dve.wait_ge(s_split, 5 * n + 1)
                    v.tensor_tensor(rest[0], of, parts[0], ALU.subtract).then_inc(s_split, 1)
                    dve.wait_ge(s_split, 5 * n + 2)
                    v.tensor_copy(parts[1], rest[0]).then_inc(s_split, 1)
                    dve.wait_ge(s_split, 5 * n + 3)
                    v.tensor_tensor(rest[1], rest[0], parts[1], ALU.subtract).then_inc(s_split, 1)
                    dve.wait_ge(s_split, 5 * n + 4)
                    v.tensor_copy(parts[2], rest[1]).then_inc(s_split, 1)
                statistics(0, 0, 0)
                moments(0, 0, 0)
                steps(dve, EG, step)
                for i in range(EG, EG + 3):
                    step(i, i % 4, i // 4)

            @block.scalar
            def _(act):
                def deviations1(i, k, h):
                    k2 = k % 2
                    wait(act, a_mv1, i + 1)
                    wait(act, a_rs1, i - 1)
                    for n, tile in enumerate((xe[k], x1n[2 * k2], x1n[2 * k2 + 1])):
                        last = s.activation(sd1[k2][:, J * n:J * n + J], by_tile(tile, XW)[:, :, MEAN + 1], ACT.Sqrt,
                                            bias=eps_col[:, :])
                    last.then_inc(a_sd1, 1)

                def store(i, k, h):
                    wait(act, a_fe, i + 1)
                    act.dma_start(block_rows(xe_d, i), xe[k][:, :]).then_inc(a_lin[k], 16)
                    for d in range(2):
                        k4 = 2 * (k % 2) + d
                        wait(act, a_fn, 2 * i + d + 1)
                        if isinstance(i, int) and 2 * i + d == NG - 1:
                            act.wait_ge(a_x1[k4 - 1], 16 * (fill2(k, h) + 1))
                        act.dma_start(rows(x1_d, 2 * i + d, XW), x1n[k4][:, :]).then_inc(a_x1[k4], 16)

                def update_relu(i, k, h):
                    wait(act, a_pre, i + 1)
                    wait(act, a_ue, i - 1)
                    s.activation(zr[k % 2][:, :], BZ[:, :], ACT.Relu, bias=c1c[:, :]).then_inc(a_zr, 1)

                def deviations(i, k, h):
                    wait(act, a_mv, i + 1)
                    wait(act, a_rs, i - 1)
                    s.activation(sd0[k % 2][:, :], mv0[k % 2][:, :, 1], ACT.Sqrt, bias=eps_col[:, :]).then_inc(a_sd, 1)

                def normalise(to, of, k, first):
                    for j in range(J):
                        m = first + j
                        last = s.activation(to[:, j * D:(j + 1) * D], of[:, j * D:(j + 1) * D], ACT.Identity,
                                            bias=nb0[k % 2][:, m:m + 1], scale=rs0[k % 2][:, J + m:J + m + 1])
                    return last

                def node_normalise(i, k, d):
                    k4 = 2 * (k % 2) + d
                    wait(act, a_ntr, 2 * i + d - 3)
                    normalise(hn[k4], xn[2 * k + d], k, J + J * d).then_inc(a_nnorm, 1)

                def node_relu(i, k, d):
                    wait(act, a_ntr, 2 * i + d + 1)
                    wait(act, a_npre, 2 * i + d - 1)
                    s.activation(tn[d][:, :], BT[d][:, :], ACT.Relu).then_inc(a_ntn, 1)

                def node_hidden(i, k, d):
                    wait(act, a_npre, 2 * i + d + 1)
                    wait(act, a_un, 2 * i + d - 3)
                    s.activation(zn[2 * (k % 2) + d][:, :], (BN, BM)[d][:, :], ACT.Relu, bias=c1c[:, :]).then_inc(a_nzn, 1)

                def message_bias(i, k, h):
                    wait(act, a_msg, i + 1)
                    wait(act, a_scan, i - 1)
                    s.activation(ms[k % 2][:, :], BM[:, :], ACT.Identity, bias=b2c[:, :]).then_inc(a_ms, 1)

                def step(i, k, h):
                    k2 = k % 2
                    if there(back(1, i, k, h)[0]):
                        message_bias(*back(1, i, k, h))
                    if there(back(3, i, k, h)[0]):
                        deviations1(*back(3, i, k, h))
                    if there(i):
                        wait(act, a_nb, i + 1)
                        wait(act, a_tr, i - 1)
                        normalise(hg[k2], xg[k][:, G:2 * G], k, 0).then_inc(a_dnorm, 1)
                        node_normalise(i, k, 0)
                        wait(act, a_tr, i + 1)
                        wait(act, a_hid, i - 1)
                        s.activation(hs[k2][:, :], BT[0][:, :], ACT.Relu)
                        wait(act, a_pre, i - 3)
                        s.activation(hd[k][:, :], BT[1][:, :], ACT.Relu).then_inc(a_relu, 1)
                        node_normalise(i, k, 1)
                    if there(back(1, i, k, h)[0]):
                        node_hidden(*back(1, i, k, h)[:2], 0)
                        node_hidden(*back(1, i, k, h)[:2], 1)
                    if there(i):
                        wait(act, a_hid, i + 1)
                        wait(act, a_msg, i - 1)
                        s.activation(ze[k2][:, :], BZ[:, :], ACT.Relu, bias=b1c[:, :]).then_inc(a_ze, 1)
                    if there(i):
                        node_relu(i, k, 0)
                        node_relu(i, k, 1)
                    if there(back(-1, i, k, h)[0]):
                        deviations(*back(-1, i, k, h))
                    if there(back(1, i, k, h)[0]):
                        update_relu(*back(1, i, k, h))
                    if there(back(3, i, k, h)[0]):
                        store(*back(3, i, k, h))
                deviations(0, 0, 0)
                steps(act, EG, step)
                for i in range(EG, EG + 3):
                    step(i, i % 4, i // 4)
                for k in range(4):
                    act.wait_ge(a_x1[k], 16 * ((EG + 1 - k // 2) // 2))
                    act.wait_ge(a_lin[k], 16 * ((EG + 3 - k) // 4))

            @block.tensor
            def _(pe):
                def times_u2(to, of):
                    mm(to[:, :], ones_bf[:, :], c2_three[:, :], start=True, stop=False)
                    for j in range(J):
                        last = mm(to[:, j * D:(j + 1) * D], of[:, j * P:(j + 1) * P], u2[:, :],
                                  start=False, stop=j == J - 1)
                    return last

                def update(i, k, h):
                    k2 = k % 2
                    wait(pe, a_zr, i + 1)
                    wait(pe, a_ge, i)
                    times_u2(BX[0], zr[k2]).then_inc(a_ue, 1)
                    for d in range(2):
                        wait(pe, a_nzn, 2 * i + d + 1)
                        wait(pe, a_ne, 2 * i + d - 1)
                        times_u2(BX[1 + d], zn[2 * k2 + d]).then_inc(a_un, 1)

                def pre(i, k, h):
                    wait(pe, a_scan, i + 1)
                    wait(pe, a_ze, min(i + 2, EG) if isinstance(i, int) else i + 2)
                    mm(BZ[:, :], u1a[:, :], hd[k][:, :], start=True, stop=False)
                    mm(BZ[:, :], u1b[:, :], scan[k % 2][:, :], start=False, stop=True).then_inc(a_pre, 1)

                def node_transpose(i, k, d):
                    wait(pe, a_nnorm, 2 * i + d + 1)
                    wait(pe, a_relu, i + 1)
                    for j in range(J):
                        last = tr(BT[d][:, j * P:(j + 1) * P], hn[2 * (k % 2) + d][:, j * D:(j + 1) * D], ident[:, :])
                    last.then_inc(a_ntr, 1)

                def node_pre(i, d):
                    wait(pe, a_ntn, 2 * i + d + 1)
                    if d == 0:
                        wait(pe, a_nzn, 2 * i - 1)
                    else:
                        wait(pe, a_ms, i + 1)
                    mm((BN, BM)[d][:, :], u1a[:, :], tn[d][:, :], start=True, stop=True).then_inc(a_npre, 1)

                def step(i, k, h):
                    k2 = k % 2
                    if there(back(2, i, k, h)[0]):
                        update(*back(2, i, k, h))
                    if there(i):
                        wait(pe, a_norm, i + 1)
                        wait(pe, a_dnorm, i + 1)
                        wait(pe, a_ntn, 2 * i)
                        for n, tile in enumerate((xg[k], hg[k2])):
                            for j in range(J):
                                last = tr(BT[n][:, j * P:(j + 1) * P], tile[:, j * D:(j + 1) * D], ident[:, :])
                        last.then_inc(a_tr, 1)
                    if there(back(1, i, k, h)[0]):
                        for d in range(2):
                            node_pre(i - 1, d)
                    if there(i):
                        wait(pe, a_relu, i + 1)
                        wait(pe, a_w[k2], 16 * fill2(k, h) + 16)
                        wait(pe, a_zr, i - 1)
                        mm(BZ[:, :], w1w9[:, :], wrow[k2][:, :], start=True, stop=False)
                        mm(BZ[:, :], w1a[:, :], hs[k2][:, :], start=False, stop=False)
                        mm(BZ[:, :], w1b[:, :], hd[k][:, :], start=False, stop=True).then_inc(a_hid, 1)
                        node_transpose(i, k, 0)
                        node_transpose(i, k, 1)
                    if there(back(1, i, k, h)[0]):
                        pre(*back(1, i, k, h))
                    if there(i):
                        wait(pe, a_ze, i + 1)
                        wait(pe, a_nzn, 2 * i)
                        mm(BM[:, :], w2[:, :], ze[k2][:, :], start=True, stop=True).then_inc(a_msg, 1)
                steps(pe, EG, step)
                for i in range(EG, EG + 2):
                    step(i, i % 4, i // 4)

        b_get, b_keep, b_share, b_xe = (sems("b_" + n, 4) for n in ("get", "keep", "share", "xe"))
        b_x = sems("b_x", 4)
        b_ae, b_an = sems("b_ae"), sems("b_an", 4)
        b_gi = sem("b_gi")
        b_norm, b_tr, b_relu, b_scan = (sem("b_" + n) for n in ("norm", "tr", "relu", "scan"))
        b_w = sem("b_w")
        b_wd = sem("b_wd")
        b_we = sem("b_we")
        b_act = sem("b_act")
        b_sc, b_nnorm, b_ntr, b_nrelu, b_nw, b_nb, b_nact, b_done = (
            sem("b_" + n) for n in ("sc", "nnorm", "ntr", "nrelu", "nw", "nb", "nact", "done"))
        BW, BD, BN = bank[2], bank[3:5], bank[5:7]

        with nc.Block() as block:
            @block.gpsimd
            def _(g):
                def step(i, k, h):
                    hold(g, b_tr, i - 3)
                    g.tensor_copy(get_idx[k][:, 0:J], src_t[:, cols(i, J)]).then_inc(b_gi, 1)
                    hold(g, b_gi, i + 1)
                    for j in range(J):
                        g.indirect_dma_start(
                            out=xg[k][:, j * XW:(j + 1) * XW], out_offset=None, in_=x1_d[:, :],
                            in_offset=bass.IndirectOffsetOnAxis(ap=get_idx[k][:, j:j + 1], axis=0),
                            bounds_check=N - 1, oob_is_err=False).then_inc(b_get[k], 16)
                steps(g, EG, step)

            @block.sync
            def _(sp):
                def step(i, k, h):
                    wait(sp, b_tr, i - 3)
                    sp.dma_start(xe[k][:, :], block_rows(xe_d, i)).then_inc(b_xe[k], 16)
                    wait(sp, b_scan, i - 3)
                    sp.dma_start(keepb[k][:, :], keep_d[cols(i, 1), :].to_broadcast([P, G])).then_inc(b_keep[k], 16)
                    wait(sp, b_wd, i - 3)
                    sp.dma_start(hd[k][:, :], share_d[cols(i, 1), :].to_broadcast([P, G])).then_inc(b_share[k], 16)
                    for d in range(2):
                        wait(sp, b_ntr, 2 * i + d - 3)
                        sp.dma_start(x1n[2 * (k % 2) + d][:, :], rows(x1_d, 2 * i + d, XW))\
                          .then_inc(b_x[2 * (k % 2) + d], 16)
                steps(sp, EG, step)

            @block.vector
            def _(dve):
                def scan_step(i, k, h):
                    wait(dve, b_relu, i + 1)
                    wait(dve, b_keep[k], 16 * h + 16)
                    wait(dve, b_w, i - 1)
                    wait(dve, b_scan, i)
                    v.tensor_tensor_scan(
                        scan[k % 2][:, :], keepb[k][:, :], hs[k % 2][:, :],
                        0.0 if isinstance(i, int) and i == 0 else scan[1 - k % 2][:, G - 1:G],
                        ALU.mult, ALU.add).then_inc(b_scan, 1)

                def degree_step(i, k, h):
                    wait(dve, b_w, i + 1)
                    wait(dve, b_share[k], 16 * h + 16)
                    wait(dve, b_we, i - 1)
                    v.tensor_tensor(ze[k % 2][:, :], BW[:, :], hd[k][:, :], ALU.mult).then_inc(b_wd, 1)

                def leaky(to, of):
                    return v.scalar_tensor_tensor(out=to[:, :], in0=of[:, :], scalar=SLOPE, in1=of[:, :],
                                                  op0=ALU.mult, op1=ALU.max)

                def statistics(slot, part):
                    to = stats[:, slot, :] if isinstance(slot, int) else stats[:, bass.ds(slot, 1), :]
                    return v.bn_stats(to, part)

                def activation(i, k, h):
                    k2 = k % 2
                    wait(dve, b_we, i + 1)
                    wait(dve, b_ae[k2], 16 * fill2(k, h))
                    leaky(zr[k2], ms[k2]).then_inc(b_act, 1)
                    for d in range(2):
                        k4 = 2 * k2 + d
                        wait(dve, b_nb, 2 * i + d + 1)
                        wait(dve, b_an[k4], 16 * fill2(k, h))
                        leaky(zn[k4], hn[k4]).then_inc(b_nact, 1)
                    hold(dve, b_act, i + 1)
                    statistics(i + NG, zr[k2][:, :]).then_inc(b_done, 1)
                    hold(dve, b_nact, 2 * i + 2)
                    for d in range(2):
                        part = zn[2 * k2 + d][:, :]
                        if isinstance(i, int) and 2 * i + d == NG - 1:
                            part = part.rearrange("p (j q) -> p j q", j=J)[:, :, DOUBLE:P]
                        statistics(2 * i + d, part).then_inc(b_done, 1)

                def normalise(i, k, h):
                    wait(dve, b_get[k], 64 * h + 64)
                    wait(dve, b_xe[k], 16 * h + 16)
                    for tile in (xg[k], xe[k]):
                        for j in range(J):
                            row, m = tile[:, j * XW:j * XW + D], j * XW + D
                            last = v.tensor_scalar(row, row, tile[:, m:m + 1], tile[:, m + 1:m + 2],
                                                   ALU.subtract, ALU.mult)
                    last.then_inc(b_norm, 1)

                def node_scales(i, k, h):
                    k2 = k % 2
                    wait(dve, b_nnorm, 2 * i - 2)
                    nodes = [by_tile(x1n[2 * k2 + d], XW) for d in range(2)]
                    for d in range(2):
                        wait(dve, b_x[2 * k2 + d], 16 * fill2(k, h) + 16)
                        v.scalar_tensor_tensor(out=rs1[k2][:, J * d:J * d + J], in0=nodes[d][:, :, DINV], scalar=1.0,
                                               in1=nodes[d][:, :, SCALE], op0=ALU.is_ge, op1=ALU.mult).then_inc(b_sc, 1)
                    wait(dve, b_sc, 4 * i + 2)
                    for d in range(2):
                        v.scalar_tensor_tensor(out=nb0[k2][:, J * d:J * d + J], in0=nodes[d][:, :, MEAN], scalar=-1.0,
                                               in1=rs1[k2][:, J * d:J * d + J], op0=ALU.mult,
                                               op1=ALU.mult).then_inc(b_sc, 1)

                def step(i, k, h):
                    if there(back(1, i, k, h)[0]):
                        scan_step(*back(1, i, k, h))
                    if there(i):
                        node_scales(i, k, h)
                    if there(back(-1, i, k, h)[0]):
                        normalise(*back(-1, i, k, h))
                    if there(back(1, i, k, h)[0]):
                        degree_step(*back(1, i, k, h))
                    if there(back(2, i, k, h)[0]):
                        activation(*back(2, i, k, h))
                normalise(0, 0, 0)
                steps(dve, EG, step)
                for i in range(EG, EG + 2):
                    step(i, i % 4, i // 4)

            @block.scalar
            def _(act):
                def edge_bias(i, k, h):
                    wait(act, b_wd, i + 1)
                    wait(act, b_act, i - 1)
                    s.activation(ms[k % 2][:, :], ze[k % 2][:, :], ACT.Identity, bias=biasc[:, :]).then_inc(b_we, 1)

                def store_edges(i, k, h):
                    wait(act, b_act, i + 1)
                    act.dma_start(block_rows(acte_d, i), zr[k % 2][:, :]).then_inc(b_ae[k % 2], 16)

                def store_nodes(i, k, h):
                    for d in range(2):
                        k4 = 2 * (k % 2) + d
                        wait(act, b_nact, 2 * i + d + 1)
                        act.dma_start(block_rows(act_d, 2 * i + d), zn[k4][:, :]).then_inc(b_an[k4], 16)

                def step(i, k, h):
                    k2 = k % 2
                    if there(back(2, i, k, h)[0]):
                        edge_bias(*back(2, i, k, h))
                    if there(i):
                        wait(act, b_tr, i + 1)
                        wait(act, b_scan, i - 1)
                        s.activation(hs[k2][:, :], bank[0][:, :], ACT.Relu)
                        wait(act, b_w, i - 1)
                        s.activation(hg[k2][:, :], bank[1][:, :], ACT.Relu).then_inc(b_relu, 1)
                        wait(act, b_sc, 4 * i + 4)
                        for d in range(2):
                            x1 = by_tile(x1n[2 * k2 + d], XW)
                            for j in range(J):
                                m = J * d + j
                                last = s.activation(x1[:, j, 0:D], x1[:, j, 0:D], ACT.Identity,
                                                    bias=nb0[k2][:, m:m + 1], scale=rs1[k2][:, m:m + 1])
                            last.then_inc(b_nnorm, 1)
                    if there(back(1, i, k, h)[0]):
                        for d in range(2):
                            b = back(1, i, k, h)
                            wait(act, b_nw, 2 * b[0] + d + 1)
                            wait(act, b_nact, 2 * b[0] + d - 3)
                            s.activation(hn[2 * (b[1] % 2) + d][:, :], BN[d][:, :], ACT.Identity,
                                         bias=biasc[:, :]).then_inc(b_nb, 1)
                    if there(i):
                        for d in range(2):
                            wait(act, b_ntr, 2 * i + d + 1)
                            wait(act, b_nw, 2 * i + d - 1)
                            s.activation(tn[d][:, :], BD[d][:, :], ACT.Relu).then_inc(b_nrelu, 1)
                    if there(back(2, i, k, h)[0]):
                        store_edges(*back(2, i, k, h))
                        store_nodes(*back(2, i, k, h))
                steps(act, EG, step)
                for i in range(EG, EG + 2):
                    step(i, i % 4, i // 4)
                for k in range(4):
                    act.wait_ge(b_an[k], 16 * ((EG + 1 - k // 2) // 2))
                for k in range(2):
                    act.wait_ge(b_ae[k], 16 * ((EG + 1 - k) // 2))

            @block.tensor
            def _(pe):
                def times_w(i, k, h):
                    wait(pe, b_scan, i + 1)
                    wait(pe, b_wd, i)
                    mm(BW[:, :], wg[:, :], hg[k % 2][:, :], start=True, stop=False)
                    mm(BW[:, :], wg[:, :], scan[k % 2][:, :], start=False, stop=True).then_inc(b_w, 1)

                def step(i, k, h):
                    if there(i):
                        wait(pe, b_norm, i + 1)
                        wait(pe, b_relu, i)
                        for n, tile in enumerate((xg[k], xe[k])):
                            for j in range(J):
                                last = tr(bank[n][:, j * P:(j + 1) * P], tile[:, j * XW:j * XW + D], ident[:, :])
                        last.then_inc(b_tr, 1)
                    if there(back(1, i, k, h)[0]):
                        times_w(*back(1, i, k, h))
                        for d in range(2):
                            wait(pe, b_nrelu, 2 * (i - 1) + d + 1)
                            wait(pe, b_nb, 2 * (i - 1) + d - 1)
                            mm(BN[d][:, :], wg[:, :], tn[d][:, :], start=True, stop=True).then_inc(b_nw, 1)
                    if there(i):
                        for d in range(2):
                            wait(pe, b_nnorm, 2 * i + d + 1)
                            wait(pe, b_nrelu, 2 * i + d - 1)
                            for j in range(J):
                                last = tr(BD[d][:, j * P:(j + 1) * P], x1n[2 * (k % 2) + d][:, j * XW:j * XW + D],
                                          ident[:, :])
                            last.then_inc(b_ntr, 1)
                steps(pe, EG, step)
                step(EG, EG % 4, EG // 4)

        o_chain, o_std, o_coef = sem("o_chain"), sem("o_std"), sem("o_coef")
        o_ld = [sems(f"o_ld{n}_", 4) for n in range(3)]
        o_st = sems("o_st", 4)
        o_put = sems("o_put", 4)
        o_pi = sem("o_pi")
        o_keep = sem("o_keep")
        o_late = sem("o_late")
        o_y, o_tr, o_sum = sem("o_y"), sem("o_tr"), sem("o_sum")
        small = {n: sb(n, [P, w_]) for n, w_ in (
            ("moments", 2), ("fill0", 1), ("fill", 1), ("off", 1), ("off2", 1), ("more", 1), ("mean", 1),
            ("dist", 1), ("dist2", 1), ("spread", 1), ("var", 1), ("std", 1), ("inv", 1), ("scale", 1),
            ("prod", 1), ("shift", 1))}
        NE = EG * G
        NALL = N + NE
        oa = [xn[0:4], xn[4:8], keepb]
        ox = [x1n, xe, [tile[:, 0:J * XW] for tile in xg]]
        oy = [hs, hg, ze]
        oo = zn

        with nc.Block() as block:
            @block.gpsimd
            def _(g):
                def scatter(i, k, h):
                    hold(g, o_put[k], 64 * h)
                    g.tensor_copy(put_idx[k][:, :], put_t[:, cols(i, J)]).then_inc(o_pi, 1)
                    hold(g, o_pi, i + 1)
                    hold(g, o_sum, 3 * i + 3)
                    with g.If(late > 0):
                        g.dma_start(block_rows(acte_d, i), hn[k][:, :]).then_inc(o_keep, 16)
                        hold(g, o_keep, 16 * i + 16)
                    for d in range(2):
                        hold(g, o_st[2 * (k % 2) + d], 16 * fill2(k, h) + 16)
                        hold(g, o_st[2 * (1 - k % 2) + d], 16 * (fill2(k, h) + k % 2))
                    for j in range(J):
                        g.indirect_dma_start(
                            out=out[:, :], in_=hn[k][:, j * D:(j + 1) * D],
                            out_offset=bass.IndirectOffsetOnAxis(ap=put_idx[k][:, j:j + 1], axis=0),
                            in_offset=None, bounds_check=N - 1, oob_is_err=False).then_inc(o_put[k], 16)
                g.wait_ge(s_flag, 4)
                late = g.value_load(any_late[0:1, 0:1])
                steps(g, EG, scatter)
                for k in range(4):
                    g.wait_ge(o_put[k], 64 * ((EG + 3 - k) // 4))
                    g.wait_ge(o_st[k], 16 * ((EG + 1 - k // 2) // 2))
                late_rows(g, out, acte_d, D, hn[0], o_late, o_pi)

            @block.sync
            def _(sp):
                def step(i, k, h):
                    for n in range(3):
                        wait(sp, o_y, 3 * (i - 4) + n + 1)
                        a = block_rows(act_d, 2 * i + n) if n < 2 else block_rows(acte_d, i)
                        sp.dma_start(oa[n][k][:, :], a).then_inc(o_ld[n][k], 16)
                        wait(sp, o_sum, 3 * (i - 4) + n + 1)
                        r = rows(x1_d, 2 * i + n, XW) if n < 2 else block_rows(xe_d, i)
                        sp.dma_start(ox[n][k][:, :], r).then_inc(o_ld[n][k], 16)
                steps(sp, EG, step)

            @block.vector
            def _(dve):
                c = {n: tile[:, :] for n, tile in small.items()}
                count = [0]

                def chained(instruction):
                    count[0] += 1
                    instruction.then_inc(o_chain, 1)
                    dve.wait_ge(o_chain, count[0])

                chained(v.bn_aggr(c["moments"], stats[:, :, :].rearrange("p t s -> p (t s)")))
                chained(v.tensor_scalar(c["fill0"], biasc[:, :], SLOPE, None, ALU.mult))
                chained(v.tensor_tensor(c["fill"], c["fill0"], biasc[:, :], ALU.max))
                chained(v.tensor_tensor(c["off"], small["moments"][:, 0:1], c["fill"], ALU.subtract))
                chained(v.scalar_tensor_tensor(out=c["mean"], in0=c["off"], scalar=NALL / N, in1=c["fill"],
                                               op0=ALU.mult, op1=ALU.add))
                chained(v.tensor_tensor(c["dist"], small["moments"][:, 0:1], c["mean"], ALU.subtract))
                chained(v.tensor_tensor(c["dist2"], c["dist"], c["dist"], ALU.mult))
                chained(v.tensor_tensor(c["spread"], c["dist2"], small["moments"][:, 1:2], ALU.add))
                chained(v.tensor_tensor(c["off"], c["fill"], c["mean"], ALU.subtract))
                chained(v.tensor_tensor(c["off2"], c["off"], c["off"], ALU.mult))
                chained(v.tensor_scalar(c["more"], c["off2"], NE / N, None, ALU.mult))
                chained(v.scalar_tensor_tensor(out=c["var"], in0=c["spread"], scalar=NALL / N, in1=c["more"],
                                               op0=ALU.mult, op1=ALU.subtract))
                dve.wait_ge(o_std, 1)
                chained(v.reciprocal(c["inv"], c["std"]))
                chained(v.tensor_tensor(c["scale"], gammac[:, :], c["inv"], ALU.mult))
                chained(v.tensor_tensor(c["prod"], c["mean"], c["scale"], ALU.mult))
                v.tensor_tensor(c["shift"], betac[:, :], c["prod"], ALU.subtract).then_inc(o_coef, 1)

                def step(i, k, h):
                    for n in range(3):
                        wait(dve, o_tr, 3 * i + n + 1)
                        wait(dve, o_ld[n][k], 32 * h + 32)
                        if n < 2:
                            k4 = 2 * (k % 2) + n
                            wait(dve, o_st[k4], 16 * fill2(k, h))
                            to = oo[k4]
                        else:
                            wait(dve, o_put[k], 64 * h)
                            to = hn[k]
                        last = v.tensor_tensor(by_tile(to, D), by_tile(bank[(3 * k + n) % 6], D),
                                               by_tile(ox[n][k], XW)[:, :, 0:D], ALU.add)
                        last.then_inc(o_sum, 1)
                steps(dve, EG, step)

            @block.scalar
            def _(act):
                act.wait_ge(o_chain, 12)
                s.activation(small["std"][:, :], small["var"][:, :], ACT.Sqrt, bias=eps_col[:, :]).then_inc(o_std, 1)
                act.wait_ge(o_coef, 1)

                def store(i, k, h):
                    for n in range(2):
                        k4 = 2 * (k % 2) + n
                        wait(act, o_sum, 3 * i + n + 1)
                        if isinstance(i, int) and 2 * i + n == NG - 1:
                            act.wait_ge(o_st[k4 - 1], 16 * (fill2(k, h) + 1))
                        act.dma_start(rows(out, 2 * i + n, D), oo[k4][:, :]).then_inc(o_st[k4], 16)

                def step(i, k, h):
                    for n in range(3):
                        y = oy[n][k % 2]
                        wait(act, o_ld[n][k], 32 * h + 32)
                        wait(act, o_tr, 3 * (i - 2) + n + 1)
                        s.activation(y[:, :], oa[n][k][:, :], ACT.Identity, bias=small["shift"][:, :],
                                     scale=small["scale"][:, :]).then_inc(o_y, 1)
                    if there(back(1, i, k, h)[0]):
                        store(*back(1, i, k, h))
                steps(act, EG, step)
                store(EG - 1, (EG - 1) % 4, (EG - 1) // 4)
                for k in range(4):
                    act.wait_ge(o_st[k], 16 * ((EG + 1 - k // 2) // 2))

            @block.tensor
            def _(pe):
                def step(i, k, h):
                    for n in range(3):
                        wait(pe, o_y, 3 * i + n + 1)
                        wait(pe, o_sum, 3 * (i - 2) + n + 1)
                        for j in range(J):
                            last = tr(bank[(3 * k + n) % 6][:, j * D:(j + 1) * D],
                                      oy[n][k % 2][:, j * P:(j + 1) * P], ident[:, :])
                        last.then_inc(o_tr, 1)
                steps(pe, EG, step)


_INPUTS = ["x", "src", "dst", "edge_weight", "L0_gnn_W1", "L0_gnn_b1", "L0_gnn_W2", "L0_gnn_b2", "L0_gnn_U1",
           "L0_gnn_c1", "L0_gnn_U2", "L0_gnn_c2", "L1_gnn_W", "L1_gnn_bias", "L1_gnn_gamma", "L1_gnn_beta"]


def kernel(**inputs):
    import numpy as np
    import concourse.bacc as bacc
    from concourse import mybir as mb
    from concourse.bass_utils import run_bass_kernel_spmd

    nc = bacc.Bacc("TRN2", target_bir_lowering=False, num_devices=1)
    arrays, args = {}, []
    for name in _INPUTS:
        a = np.ascontiguousarray(inputs[name])
        arrays[f"in_{name}"] = a
        args.append(nc.dram_tensor(f"in_{name}", a.shape, mb.dt.from_np(a.dtype), kind="ExternalInput").ap())
    out = nc.dram_tensor("out_x", arrays["in_x"].shape, mb.dt.float32, kind="ExternalOutput").ap()
    gnn_kernel(nc, *args, out)
    r = run_bass_kernel_spmd(nc, [arrays], core_ids=[0])
    return r.results[0]["out_x"]
```

```python
from contextlib import ExitStack

import concourse.bass as bass
from concourse import mybir

F32 = mybir.dt.float32
BF16 = mybir.dt.bfloat16
I32 = mybir.dt.int32
ALU = mybir.AluOpType
ACT = mybir.ActivationFunctionType
AXIS_X, AXIS_C = mybir.AxisListType.X, mybir.AxisListType.C

P = 128
D = 128
J = 4
G = P * J
LN_EPS = 1e-5
BN_EPS = 1e-5
SLOPE = 0.01
XW = D + 3
MEAN, SCALE, DINV = D, D + 1, D + 2
RESTART = 1e30


def gnn_kernel(nc, x, src, dst, w, W1, b1, W2, b2, U1, c1, U2, c2, W, bias, gamma, beta, out):
    N = x.shape[0]
    E = src.shape[0]
    EG = -(-E // G)
    ET = EG * J
    NG = -(-N // G)
    LAST_BASE = N - G
    DOUBLE = ((NG - 1) * G - LAST_BASE) // J
    assert NG == 2 * EG and EG % 2 == 1 and ((NG - 1) * G - LAST_BASE) % J == 0
    EC = 2 * P
    EQ = EG * G // EC
    EFULL = E // EC
    EREST = E - EFULL * EC
    assert EQ == EFULL + 1 and EREST > 1
    KEPT = 13
    NOWHERE = 2 * N
    SORT_C = 28
    SORT_W = EG * G // SORT_C
    sorted_d = [nc.dram_tensor(n, (E, 1), dt, kind="Internal").ap()
                for n, dt in (("src_s", I32), ("dst_s", I32), ("w_s", F32))]
    key_d = nc.dram_tensor("key_d", (EG * G, 1), F32, kind="Internal").ap()
    rank_d = nc.dram_tensor("rank_d", (EG * G, 1), F32, kind="Internal").ap()
    x1_d = nc.dram_tensor("x1_d", (N, XW), F32, kind="Internal").ap()
    xe_d = nc.dram_tensor("xe_d", (EG * P, J * XW), F32, kind="Internal").ap()
    act_d = nc.dram_tensor("act_d", (NG * P, G), F32, kind="Internal").ap()
    acte_d = nc.dram_tensor("acte_d", (EG * P, G), F32, kind="Internal").ap()
    pen_d = nc.dram_tensor("pen_d", (EG, G), F32, kind="Internal").ap()
    keep_d = nc.dram_tensor("keep_d", (EG, G), F32, kind="Internal").ap()
    share_d = nc.dram_tensor("share_d", (EG, G), F32, kind="Internal").ap()
    w_d = nc.dram_tensor("w_d", (EQ, 9, EC), BF16, kind="Internal").ap()

    def rows(table, t, width):
        if isinstance(t, int):
            base = min(t * G, LAST_BASE)
            part = table[base:base + G, 0:width]
        else:
            part = table[bass.ds(t * G, G), 0:width]
        return part.rearrange("(p j) f -> p (j f)", j=J)

    def block_rows(table, t):
        return table[bass.ds(t * P, P), :] if not isinstance(t, int) else table[t * P:(t + 1) * P, :]

    def cols(t, n):
        return bass.ds(t * n, n) if not isinstance(t, int) else slice(t * n, (t + 1) * n)

    ctx = ExitStack()
    with ctx:
        def sb(name, shape, dt=F32):
            return ctx.enter_context(nc.sbuf_tensor(name, shape, dt))

        def sem(name):
            return ctx.enter_context(nc.semaphore(name))

        def sems(name, n=2):
            return [sem(f"{name}{k}") for k in range(n)]

        ident = sb("ident", [P, P])
        ones_row = sb("ones_row", [1, P])
        w1a, w1b, w2 = sb("w1a", [P, D]), sb("w1b", [P, D]), sb("w2", [P, D])
        u1a, u1b, u2, wg = sb("u1a", [P, D]), sb("u1b", [P, D]), sb("u2", [P, D]), sb("wg", [P, D])
        w1w = sb("w1w", [1, D])
        w1w_parts = [sb(f"w1w_part{n}", [1, D], BF16) for n in range(3)]
        w1w9 = sb("w1w9", [9, D], BF16)
        b1c, b2c, c1c, biasc = sb("b1c", [P, 1]), sb("b2c", [P, 1]), sb("c1c", [P, 1]), sb("biasc", [P, 1])
        gammac, betac = sb("gammac", [P, 1]), sb("betac", [P, 1])
        eps_col, one_col = sb("eps_col", [P, 1]), sb("one_col", [P, 1])
        c2_row = sb("c2_row", [1, G])
        c2_parts = [sb(f"c2_part{n}", [1, G], BF16) for n in range(3)]
        c2_three = sb("c2_three", [3, G], BF16)
        ones_bf = sb("ones_bf", [3, P], BF16)
        src_t, dst_t, put_t = sb("src_t", [P, ET], I32), sb("dst_t", [P, ET], I32), sb("put_t", [P, ET], I32)
        late_t = sb("late_t", [P, ET], I32)
        count_t, dinv_t = sb("count_t", [P, ET]), sb("dinv_t", [P, ET])
        stats = sb("stats", [P, NG + EG, 6])

        def ring(name, shape, n=2, dt=F32):
            return [sb(f"{name}{k}", shape, dt) for k in range(n)]

        xg = ring("xg", [P, 2 * J * XW], 4)
        hg = ring("hg", [P, G])
        hs, hd = ring("hs", [P, G]), ring("hd", [P, G], 4)
        ze, ms = ring("ze", [P, G]), ring("ms", [P, G])
        scan = ring("scan", [P, G])
        keepb = ring("keepb", [P, G], 4)
        wrow = ring("wrow", [9, G], 2, BF16)
        zr = ring("zr", [P, G])
        xe = ring("xe", [P, J * XW], 4)
        get_idx = ring("get_idx", [P, 2 * J], 4, I32)
        put_idx = ring("put_idx", [P, J], 4, I32)
        xn = ring("xn", [P, G], 8)
        hn = ring("hn", [P, G], 4)
        tn = ring("tn", [P, G])
        zn = ring("zn", [P, G], 4)
        x1n = ring("x1n", [P, J * XW], 4)
        st0, mv0, sd0, rs0 = (ring(n, [P, 16] + w_) for n, w_ in (("st0", [6]), ("mv0", [2]), ("sd0", []), ("rs0", [])))
        nb0 = ring("nb0", [P, 3 * J])
        st1, sd1, rs1 = (ring(n, [P, 12] + w_) for n, w_ in (("st1", [6]), ("sd1", []), ("rs1", [])))

        bank = [ctx.enter_context(nc.psum_tensor(f"bank{k}", [P, 512], F32)) for k in range(8)]

        any_late = sb("any_late", [1, 1], I32)

        setup_ctx = ExitStack()

        def tmp(name, shape, dt=F32):
            return setup_ctx.enter_context(nc.sbuf_tensor(name, shape, dt))

        def tmp_ring(name, shape, n=2, dt=F32):
            return [tmp(f"{name}{k}", shape, dt) for k in range(n)]

        dst_a, prev_a, next_a, src_a = (tmp(n, [P, EC], I32) for n in ("dst_a", "prev_a", "next_a", "src_a"))
        w_a = tmp("w_a", [P, EC])
        pen_a, keep_a, local_a, allkeep_a, count_a, put_a = (
            tmp(n, [P, EC]) for n in ("pen_a", "keep_a", "local_a", "allkeep_a", "count_a", "put_a"))
        srcf_a, dstf_a, same_a = tmp("srcf_a", [P, EC]), tmp("dstf_a", [P, EC]), tmp("same_a", [P, EC])
        ones_a, zeros_a = tmp("ones_a", [P, EC]), tmp("zeros_a", [P, EC])
        ends_r = tmp("ends_r", [1, 2 * EQ])
        carry_r = tmp("carry_r", [1, EQ + 1])
        carry_c = tmp("carry_c", [P, 1])
        share_a, deg_a = tmp("share_a", [P, EC]), tmp("deg_a", [P, EC])
        rest_row = tmp_ring("rest_row", [1, G])
        rest_a = tmp_ring("rest_a", [P, EC])
        w_parts = tmp_ring("w_part", [P, EC], 3, BF16)

        place_i = tmp("place_i", [P, SORT_W], I32)
        place_f, bkey, hit, hits = (tmp(n, [P, SORT_W]) for n in ("place_f", "bkey", "hit", "hits"))
        edge_i, edge_f, key_c, rank_c = (tmp("edge_i", [P, 1], I32), tmp("edge_f", [P, 1]),
                                          tmp("key_c", [P, 1]), tmp("rank_c", [P, 1]))
        key_t = tmp("key_t", [P, ET])
        rank_r, rank_i = tmp("rank_r", [1, SORT_W]), tmp("rank_i", [P, 1], I32)
        own = [tmp(f"own{n}", [P, 1], dt) for n, dt in enumerate((I32, I32, F32))]
        key_a, misorder_a = tmp("key_a", [P, EC]), tmp("misorder_a", [P, EC])
        misorders_f, misorders = tmp("misorders_f", [1, 1]), tmp("misorders", [1, 1], I32)

        s_order = sem("s_order")
        s_seen = sem("s_seen")
        s_sort = sem("s_sort")
        s_sorted = sem("s_sorted")
        s_blank = sem("s_blank")
        s_fill = sem("s_fill")
        s_weights = sem("s_weights")
        s_edges = sem("s_edges")
        bound_i, bound_f = tmp("bound_i", [P, 1], I32), tmp("bound_f", [P, 1])
        above_a, late_a, now_a = (tmp(n, [P, EC]) for n in ("above_a", "late_a", "now_a"))
        s_bound = sem("s_bound")
        s_late = sem("s_late")
        islate_a = tmp("islate_a", [P, EC])
        lates_r, upto_r = tmp("lates_r", [1, EC]), tmp("upto_r", [1, EC])
        s_flag = sem("s_flag")
        s_split = sem("s_split")
        s_deg = sem("s_deg")
        s_id = sem("s_id")
        s_arr = sem("s_arr")
        s_ends = sem("s_ends")
        s_carry = sem("s_carry")
        s_tr = sem("s_tr")
        s_tv = sem("s_tv")
        s_dv = sem("s_dv")
        s_masks = sem("s_masks")

        def col(v):
            return v.rearrange("(p o) -> p o", o=1)

        weight_loads = [
            (w1a[:, :], W1[0:D, :]), (w1b[:, :], W1[D:2 * D, :]), (w1w[:, :], W1[2 * D:2 * D + 1, :]),
            (w2[:, :], W2[:, :]), (u1a[:, :], U1[0:D, :]), (u1b[:, :], U1[D:2 * D, :]),
            (u2[:, :], U2[:, :]), (wg[:, :], W[:, :]),
            (b1c[:, :], col(b1)), (b2c[:, :], col(b2)), (c1c[:, :], col(c1)), (biasc[:, :], col(bias)),
            (gammac[:, :], col(gamma)), (betac[:, :], col(beta)),
        ] + [(c2_row[:, j * D:(j + 1) * D], c2.rearrange("(o f) -> o f", o=1)) for j in range(J)]
        N_WEIGHTS = len(weight_loads)

        s_held = sem("s_held")
        def wait(eng, signal, value):
            if not isinstance(value, int) or value > 0:
                eng.wait_ge(signal, value)

        def hold(eng, signal, value):
            if not isinstance(value, int) or value > 0:
                eng.wait_ge(signal, value)
                eng.sem_inc(s_held, 1)

        def steps(eng, n, step, first=8, last=1):
            assert first % 4 == 0 and (n - last) % 4 == 0
            for i in range(first):
                step(i, i % 4, i // 4)
            with eng.Fori(first // 4, (n - last) // 4) as h:
                for k in range(4):
                    step(4 * h + k, k, h)
            for i in range(n - last, n):
                step(i, i % 4, i // 4)

        def back(n, i, k, h):
            return i - n, (k - n) % 4, h + (k - n) // 4

        def there(i):
            return not isinstance(i, int) or 0 <= i < EG

        def fill2(k, h):
            return 2 * h + k // 2

        def by_tile(tile, width):
            return tile[:, :].rearrange("p (j a) -> p j a", a=width)

        a_get = sems("a_get", 4)
        a_gi = sem("a_gi")
        a_tr = sem("a_tr")
        a_ge = sem("a_ge")

        def place_indices(i, k):
            nc.vector.tensor_copy(get_idx[k][:, 0:J], src_t[:, cols(i, J)]).then_inc(a_gi, 1)
            nc.vector.tensor_copy(get_idx[k][:, J:2 * J], dst_t[:, cols(i, J)]).then_inc(a_gi, 1)

        def gather(g, i, k, h):
            hold(g, a_tr, i - 3)
            hold(g, a_ge, i - 3)
            hold(g, a_gi, 2 * i + 2)
            for j in range(2 * J):
                g.indirect_dma_start(
                    out=xg[k][:, j * D:(j + 1) * D], out_offset=None, in_=x[:, :],
                    in_offset=bass.IndirectOffsetOnAxis(ap=get_idx[k][:, j:j + 1], axis=0),
                    bounds_check=N - 1, oob_is_err=False).then_inc(a_get[k], 16)

        def flat(v, a, b):
            return v[a:b].rearrange("(q c) -> q c", c=EC)

        def line(v, a, b):
            return v[a:b].rearrange("(q c) -> q c", q=1)

        def load_edges(eng, tile, v, signal):
            eng.dma_start(tile[0:EFULL, :], flat(v, 0, EFULL * EC)).then_inc(signal, 16)
            eng.dma_start(tile[EFULL:EQ, 0:EREST], line(v, EFULL * EC, E)).then_inc(signal, 16)

        def load_before(eng, v, signal):
            full = EFULL * EC
            eng.dma_start(prev_a[0:1, 1:EC], line(v, 0, EC - 1)).then_inc(signal, 16)
            eng.dma_start(prev_a[1:EFULL, :], flat(v, EC - 1, full - 1)).then_inc(signal, 16)
            eng.dma_start(prev_a[EFULL:EQ, 0:EREST], line(v, full - 1, E - 1)).then_inc(signal, 16)

        def sort_edges(g):
            count = [0]

            def step(instruction):
                count[0] += 1
                instruction.then_inc(s_sort, 1)
                g.wait_ge(s_sort, count[0])

            step(g.iota(place_i[:, :], pattern=[[1, SORT_W]], base=0, channel_multiplier=0))
            step(g.tensor_copy(place_f[:, :], place_i[:, :]))
            step(g.iota(edge_i[:, :], pattern=[[0, 1]], base=0, channel_multiplier=1))
            step(g.tensor_scalar(key_a[0:EQ, :], dst_a[0:EQ, :], 2.0, None, ALU.mult))
            g.dma_start(key_d.rearrange("(q c) o -> q (c o)", c=EC), key_a[0:EQ, :]).then_inc(s_seen, 16)
            hold(g, s_seen, 16 * 4)
            with g.Fori(0, ET) as t:
                g.dma_start(key_t[:, bass.ds(t, 1)], key_d[bass.ds(t * P, P), :]).then_inc(s_seen, 16)
                hold(g, s_seen, 16 * t + 16 * 5)
            BEFORE = 16 * (4 + ET)
            STEPS, DMAS = 4 + 6 * ET, 16 * 2

            with g.Fori(0, SORT_C) as c:
                steps0, dmas0 = c * STEPS + count[0], c * DMAS + BEFORE
                chunk = key_d[bass.ds(c * SORT_W, SORT_W), :].rearrange("(q e) o -> q (e o)", q=1)
                g.dma_start(bkey[:, :], chunk.to_broadcast([P, SORT_W])).then_inc(s_seen, 16)
                g.memset(hits[:, :], 0.0).then_inc(s_sort, 1)
                g.tensor_copy(edge_f[:, :], edge_i[:, :]).then_inc(s_sort, 1)
                hold(g, s_sort, steps0 + 2)
                hold(g, s_seen, dmas0 + 16)
                with g.Fori(0, ET) as t:
                    first = steps0 + 6 * t + 3
                    g.tensor_copy(key_c[:, :], key_t[:, bass.ds(t, 1)]).then_inc(s_sort, 1)
                    hold(g, s_sort, first)
                    g.tensor_scalar(hit[:, :], place_f[:, :], edge_f[:, :], key_c[:, :],
                                    ALU.is_le, ALU.add).then_inc(s_sort, 1)
                    hold(g, s_sort, first + 1)
                    g.tensor_tensor(hit[:, :], hit[:, :], bkey[:, :], ALU.subtract).then_inc(s_sort, 1)
                    hold(g, s_sort, first + 2)
                    g.tensor_scalar(hit[:, :], hit[:, :], 0.0, None, ALU.is_le).then_inc(s_sort, 1)
                    hold(g, s_sort, first + 3)
                    g.tensor_tensor(hits[:, :], hits[:, :], hit[:, :], ALU.add).then_inc(s_sort, 1)
                    g.tensor_scalar(edge_f[:, :], edge_f[:, :], float(P), None, ALU.add).then_inc(s_sort, 1)
                    hold(g, s_sort, first + 5)
                g.tensor_reduce(rank_r[:, :], hits[:, :], AXIS_C, ALU.add).then_inc(s_sort, 1)
                g.tensor_scalar(place_f[:, :], place_f[:, :], float(SORT_W), None, ALU.add).then_inc(s_sort, 1)
                hold(g, s_sort, steps0 + STEPS)
                g.dma_start(rank_d[bass.ds(c * SORT_W, SORT_W), :].rearrange("(q e) o -> q (e o)", q=1),
                            rank_r[:, :]).then_inc(s_seen, 16)
                hold(g, s_seen, dmas0 + DMAS)
            steps1, dmas1 = count[0] + SORT_C * STEPS, BEFORE + SORT_C * DMAS

            def tile(t, n):
                at = bass.ds(t * P, n) if not isinstance(t, int) else slice(t * P, t * P + n)
                for to, of in zip(own, (src, dst, w)):
                    g.dma_start(to[0:n, :], of[at].rearrange("(p o) -> p o", o=1)).then_inc(s_seen, 16)
                g.dma_start(rank_c[0:n, :], rank_d[at, :]).then_inc(s_seen, 16)
                hold(g, s_seen, dmas1 + 16 * 7 * t + 16 * 4)
                g.tensor_copy(rank_i[0:n, :], rank_c[0:n, :]).then_inc(s_sort, 1)
                hold(g, s_sort, steps1 + t + 1)
                for to, of in zip(sorted_d, own):
                    g.indirect_dma_start(
                        out=to[:, :], in_=of[0:n, :],
                        out_offset=bass.IndirectOffsetOnAxis(ap=rank_i[0:n, 0:1], axis=0),
                        in_offset=None, bounds_check=E - 1, oob_is_err=False).then_inc(s_seen, 16)
                hold(g, s_seen, dmas1 + 16 * 7 * t + 16 * 7)

            with g.Fori(0, E // P) as t:
                tile(t, P)
            if E % P:
                tile(E // P, E % P)

        with nc.Block() as block:
            @block.gpsimd
            def _(g):
                g.memset(dst_a[:, :], N).then_inc(s_blank, 1)
                g.memset(prev_a[:, :], -1).then_inc(s_blank, 1)
                g.memset(next_a[:, :], N).then_inc(s_blank, 1)
                g.memset(src_a[:, :], 0).then_inc(s_blank, 1)
                g.memset(w_a[:, :], 0.0).then_inc(s_blank, 1)
                g.iota(bound_i[:, :], pattern=[[0, 1]], base=G, channel_multiplier=G).then_inc(s_bound, 1)
                g.memset(ident[:, :], 0.0).then_inc(s_id, 1)
                g.wait_ge(s_id, 1)
                g.affine_select(out=ident[:, :], in_=ident[:, :], compare_op=ALU.not_equal, fill=1.0,
                                base=0, pattern=[[-1, P]], channel_multiplier=1).then_inc(s_id, 1)
                for to, of in zip(sorted_d, (src, dst, w)):
                    g.dma_start(to.rearrange("e o -> (e o)"), of[:]).then_inc(s_seen, 16)
                g.wait_ge(s_seen, 16 * 3)
                g.wait_ge(s_order, 4)
                unsorted = g.value_load(misorders[0:1, 0:1])
                with g.If(unsorted > 0):
                    sort_edges(g)
                g.sem_inc(s_sorted, 1)
                gather(g, 0, 0, 0)

            @block.sync
            def _(sp):
                by_dst = [v.rearrange("e o -> (e o)") for v in sorted_d]
                full = EFULL * EC
                sp.wait_ge(s_blank, 5)
                load_edges(sp, dst_a, dst, s_edges)
                load_before(sp, dst, s_edges)
                sp.wait_ge(s_sorted, 1)
                for tile, v in zip((src_a, dst_a, w_a), by_dst):
                    load_edges(sp, tile, v, s_edges)
                load_before(sp, by_dst[1], s_edges)
                sp.dma_start(next_a[0:EFULL, :], flat(by_dst[1], 1, full + 1)).then_inc(s_edges, 16)
                sp.dma_start(next_a[EFULL:EQ, 0:EREST - 1], line(by_dst[1], full + 1, E)).then_inc(s_edges, 16)
                sp.wait_ge(s_edges, 16 * 16)
                sp.wait_ge(s_arr, 2)
                sp.dma_start(pen_d.rearrange("s (h c) -> (s h) c", c=EC), pen_a[0:EQ, :]).then_inc(s_masks, 16)
                sp.dma_start(keep_d.rearrange("s (h c) -> (s h) c", c=EC), keep_a[0:EQ, :]).then_inc(s_masks, 16)
                sp.wait_ge(s_dv, 6)
                sp.dma_start(share_d.rearrange("s (h c) -> (s h) c", c=EC), share_a[0:EQ, :]).then_inc(s_masks, 16)
                sp.wait_ge(s_weights, 16 * N_WEIGHTS)

            @block.scalar
            def _(act):
                for to, of in weight_loads:
                    act.dma_start(to, of).then_inc(s_weights, 16)
                act.wait_ge(s_arr, 12)
                nc.scalar.activation(deg_a[0:EQ, :], count_a[0:EQ, :], ACT.Sqrt, bias=one_col[0:EQ, :]).then_inc(s_deg, 1)
                act.wait_ge(s_tv, 5)
                nc.scalar.activation(dinv_t[:, :], count_t[:, :], ACT.Sqrt, bias=one_col[:, :]).then_inc(s_deg, 1)

            @block.vector
            def _(dve):
                v = nc.vector

                def indices(k, to):
                    dve.wait_ge(s_tr, k + 1)
                    v.tensor_copy(to[:, :].rearrange("p (q h) -> p h q", h=2),
                                  bank[2 + k][:, 0:2 * EQ].rearrange("p (h q) -> p h q", h=2)).then_inc(s_tv, 1)

                v.memset(ones_a[:, :], 1.0).then_inc(s_fill, 1)
                v.memset(zeros_a[:, :], 0.0).then_inc(s_fill, 1)
                v.memset(eps_col[:, :], LN_EPS).then_inc(s_fill, 1)
                v.memset(one_col[:, :], 1.0).then_inc(s_fill, 1)
                v.memset(ones_row[:, :], 1.0).then_inc(s_fill, 1)
                v.memset(carry_r[:, :], 0.0).then_inc(s_fill, 1)
                dve.wait_ge(s_edges, 16 * 5)
                v.tensor_tensor(misorder_a[0:EQ, :], prev_a[0:EQ, :], dst_a[0:EQ, :], ALU.is_gt).then_inc(s_order, 1)
                dve.wait_ge(s_order, 2)
                v.tensor_reduce(misorders_f[:, :], bank[7][0:1, 0:EC], AXIS_X, ALU.add).then_inc(s_order, 1)
                dve.wait_ge(s_order, 3)
                v.tensor_copy(misorders[:, :], misorders_f[:, :]).then_inc(s_order, 1)
                dve.wait_ge(s_edges, 16 * 16)
                dve.wait_ge(s_fill, 6)
                q = slice(0, EQ)
                v.tensor_tensor(same_a[q, :], prev_a[q, :], dst_a[q, :], ALU.subtract).then_inc(s_dv, 1)
                dve.wait_ge(s_dv, 1)
                v.tensor_scalar(pen_a[q, :], same_a[q, :], RESTART, None, ALU.mult).then_inc(s_arr, 1)
                v.tensor_scalar(keep_a[q, :], same_a[q, :], 0.0, None, ALU.is_equal).then_inc(s_arr, 1)
                dve.wait_ge(s_arr, 2)
                v.tensor_tensor_scan(local_a[q, :], keep_a[q, :], ones_a[q, :], 0.0, ALU.mult, ALU.add).then_inc(s_arr, 1)
                v.tensor_tensor_scan(allkeep_a[q, :], keep_a[q, :], zeros_a[q, :], 1.0, ALU.mult, ALU.add).then_inc(s_arr, 1)
                v.tensor_copy(srcf_a[q, :], src_a[q, :]).then_inc(s_arr, 1)
                v.tensor_copy(dstf_a[q, :], dst_a[q, :]).then_inc(s_arr, 1)
                v.tensor_copy(count_a[q, :], next_a[q, :]).then_inc(s_arr, 1)
                dve.wait_ge(s_arr, 7)
                v.tensor_tensor(same_a[q, :], count_a[q, :], dstf_a[q, :], ALU.is_equal).then_inc(s_arr, 1)
                dve.wait_ge(s_arr, 8)
                v.scalar_tensor_tensor(out=put_a[q, :], in0=same_a[q, :], scalar=float(NOWHERE), in1=dstf_a[q, :],
                                       op0=ALU.mult, op1=ALU.add).then_inc(s_arr, 1)
                indices(0, src_t)
                indices(1, dst_t)
                dve.wait_ge(s_tv, 2)
                for i in range(3):
                    place_indices(i, i)
                dve.wait_ge(s_bound, 1)
                v.tensor_copy(bound_f[:, :], bound_i[:, :]).then_inc(s_late, 1)
                dve.wait_ge(s_late, 1)
                v.tensor_scalar(above_a[q, :], dstf_a[q, :], bound_f[q, :], float(NOWHERE),
                                ALU.is_ge, ALU.mult).then_inc(s_late, 1)
                dve.wait_ge(s_late, 2)
                dve.wait_ge(s_arr, 9)
                v.scalar_tensor_tensor(out=late_a[q, :], in0=put_a[q, :], scalar=float(NOWHERE), in1=above_a[q, :],
                                       op0=ALU.add, op1=ALU.subtract).then_inc(s_late, 1)
                v.tensor_tensor(now_a[q, :], put_a[q, :], above_a[q, :], ALU.add).then_inc(s_late, 1)
                dve.wait_ge(s_late, 4)
                v.tensor_scalar(islate_a[q, :], late_a[q, :], float(N), None, ALU.is_lt).then_inc(s_late, 1)
                dve.wait_ge(s_ends, 1)
                v.tensor_copy(ends_r[:, :], bank[0][0:1, 0:2 * EQ]).then_inc(s_arr, 1)
                dve.wait_ge(s_arr, 10)
                v.tensor_tensor_scan(carry_r[:, 1:EQ + 1], ends_r[:, EQ:2 * EQ], ends_r[:, 0:EQ], 0.0,
                                     ALU.mult, ALU.add).then_inc(s_arr, 1)
                dve.wait_ge(s_carry, 1)
                v.tensor_copy(carry_c[q, :], bank[1][q, 0:1]).then_inc(s_dv, 1)
                dve.wait_ge(s_dv, 2)
                v.scalar_tensor_tensor(out=count_a[q, :], in0=allkeep_a[q, :], scalar=carry_c[q, :], in1=local_a[q, :],
                                       op0=ALU.mult, op1=ALU.add).then_inc(s_arr, 1)
                for k, to in ((2, put_t), (3, late_t), (4, count_t)):
                    indices(k, to)
                dve.wait_ge(s_flag, 1)
                v.tensor_copy(lates_r[:, :], bank[7][0:1, 0:EC]).then_inc(s_flag, 1)
                dve.wait_ge(s_flag, 2)
                v.tensor_tensor_scan(upto_r[:, :], ones_a[0:1, :], lates_r[:, :], 0.0, ALU.mult, ALU.add).then_inc(s_flag, 1)
                dve.wait_ge(s_flag, 3)
                v.tensor_copy(any_late[:, :], upto_r[:, EC - 1:EC]).then_inc(s_flag, 1)
                dve.wait_ge(s_deg, 2)
                v.reciprocal(dinv_t[:, :], dinv_t[:, :]).then_inc(s_dv, 1)
                v.reciprocal(share_a[q, :], deg_a[q, :]).then_inc(s_dv, 1)
                dve.wait_ge(s_dv, 4)
                v.tensor_tensor(deg_a[q, :], share_a[q, :], same_a[q, :], ALU.mult).then_inc(s_dv, 1)
                dve.wait_ge(s_dv, 5)
                v.tensor_tensor(share_a[q, :], share_a[q, :], deg_a[q, :], ALU.subtract).then_inc(s_dv, 1)
                for tile in x1n:
                    v.memset(tile[:, :].rearrange("p (j a) -> p j a", a=XW)[:, :, DINV], 1.0).then_inc(s_fill, 1)

            @block.tensor
            def _(pe):
                def transposed(k, of):
                    for h in range(2):
                        last = nc.tensor.transpose(bank[2 + k][:, h * EQ:(h + 1) * EQ],
                                                   of[0:EQ, h * P:(h + 1) * P], ident[0:EQ, 0:EQ])
                    last.then_inc(s_tr, 1)

                pe.wait_ge(s_fill, 6)
                pe.wait_ge(s_order, 1)
                nc.tensor.matmul(bank[7][0:1, 0:EC], one_col[0:EQ, :], misorder_a[0:EQ, :],
                                 start=True, stop=True).then_inc(s_order, 1)
                pe.wait_ge(s_id, 2)
                pe.wait_ge(s_arr, 4)
                for k, of in enumerate((local_a, allkeep_a)):
                    last = nc.tensor.matmul(bank[0][0:1, k * EQ:(k + 1) * EQ], of[0:EQ, EC - 1:EC],
                                            ident[0:EQ, 0:EQ], start=True, stop=True)
                last.then_inc(s_ends, 1)
                pe.wait_ge(s_arr, 6)
                transposed(0, srcf_a)
                transposed(1, dstf_a)
                pe.wait_ge(s_arr, 11)
                nc.tensor.matmul(bank[1][0:EQ, 0:1], carry_r[:, 0:EQ], ones_row[:, 0:1],
                                 start=True, stop=True).then_inc(s_carry, 1)
                pe.wait_ge(s_late, 4)
                transposed(2, now_a)
                transposed(3, late_a)
                pe.wait_ge(s_arr, 12)
                transposed(4, count_a)
                pe.wait_ge(s_late, 5)
                nc.tensor.matmul(bank[7][0:1, 0:EC], one_col[0:EQ, :], islate_a[0:EQ, :],
                                 start=True, stop=True).then_inc(s_flag, 1)

        def late_rows(g, table, of, width, landing, signal, indexed):
            g.wait_ge(s_flag, 4)
            late = g.value_load(any_late[0:1, 0:1])
            with g.If(late > 0):
                with g.Fori(0, EG) as i:
                    g.dma_start(landing[:, :], block_rows(of, i)).then_inc(signal, 16)
                    g.tensor_copy(put_idx[0][:, :], late_t[:, cols(i, J)]).then_inc(indexed, 1)
                    hold(g, signal, 80 * i + 16)
                    hold(g, indexed, EG + i + 1)
                    for j in range(J):
                        g.indirect_dma_start(
                            out=table[:, :], in_=landing[:, j * width:(j + 1) * width],
                            out_offset=bass.IndirectOffsetOnAxis(ap=put_idx[0][:, j:j + 1], axis=0),
                            in_offset=None, bounds_check=N - 1, oob_is_err=False).then_inc(signal, 16)
                    hold(g, signal, 80 * i + 80)
        v, s, mm, tr = nc.vector, nc.scalar, nc.tensor.matmul, nc.tensor.transpose

        a_mask = sems("a_mask", 4)
        a_w = sems("a_w")
        a_put = sems("a_put", 4)
        a_lin = sems("a_lin", 4)
        a_x = sems("a_x", 8)
        a_x1 = sems("a_x1", 4)
        a_late = sem("a_late")
        a_pi = sem("a_pi")
        a_st, a_mv, a_sd, a_rs, a_nb = (sem("a_" + n) for n in ("st", "mv", "sd", "rs", "nb"))
        a_norm, a_dnorm = sem("a_norm"), sem("a_dnorm")
        a_relu = sem("a_relu")
        a_hid = sem("a_hid")
        a_ze = sem("a_ze")
        a_msg = sem("a_msg")
        a_ms = sem("a_ms")
        a_scan = sem("a_scan")
        a_pre = sem("a_pre")
        a_zr = sem("a_zr")
        a_nnorm, a_ntr, a_ntn, a_npre, a_nzn = (sem("a_" + n) for n in ("nnorm", "ntr", "ntn", "npre", "nzn"))
        a_ue, a_un = sem("a_ue"), sem("a_un")
        a_ne = sem("a_ne")
        a_st1, a_mv1, a_sd1, a_rs1 = (sem("a_" + n) for n in ("st1", "mv1", "sd1", "rs1"))
        a_fe, a_fn = sem("a_fe"), sem("a_fn")
        BT, BZ, BM, BN, BX = bank[0:2], bank[2], bank[3], bank[4], bank[5:8]

        with nc.Block() as block:
            @block.gpsimd
            def _(g):
                def scatter(i, k, h):
                    hold(g, a_pi, i + 1)
                    hold(g, a_fe, i + 1)
                    for d in range(2):
                        hold(g, a_x1[2 * (k % 2) + d], 16 * fill2(k, h) + 16)
                    for j in range(J):
                        g.indirect_dma_start(
                            out=x1_d[:, :], in_=xe[k][:, j * XW:(j + 1) * XW],
                            out_offset=bass.IndirectOffsetOnAxis(ap=put_idx[k][:, j:j + 1], axis=0),
                            in_offset=None, bounds_check=N - 1, oob_is_err=False).then_inc(a_put[k], 16)

                def step(i, k, h):
                    if not isinstance(i, int) or i > 0:
                        gather(g, i, k, h)
                    if there(back(6, i, k, h)[0]):
                        scatter(*back(6, i, k, h))
                steps(g, EG, step)
                for i in range(EG - 6, EG):
                    scatter(i, i % 4, i // 4)
                for k in range(4):
                    g.wait_ge(a_put[k], 64 * ((EG + 3 - k) // 4))
                    g.wait_ge(a_lin[k], 16 * ((EG + 3 - k) // 4))
                    g.wait_ge(a_x1[k], 16 * ((EG + 1 - k // 2) // 2))
                late_rows(g, x1_d, xe_d, XW, xe[0], a_late, a_pi)

            @block.sync
            def _(sp):
                def nodes(i, k):
                    for d in range(2):
                        wait(sp, a_ne, 2 * (i - 4) + d + 1)
                        sp.dma_start(xn[2 * k + d][:, :], rows(x, 2 * i + d, D)).then_inc(a_x[2 * k + d], 16)

                def step(i, k, h):
                    if not isinstance(i, int) or i > 1:
                        nodes(i, k)
                    k2 = k % 2
                    wait(sp, a_scan, i - 3)
                    sp.dma_start(keepb[k][:, :], pen_d[cols(i, 1), :].to_broadcast([P, G])).then_inc(a_mask[k], 16)
                    wait(sp, a_hid, i - 1)
                    sp.dma_start(wrow[k2][:, :], w_d[cols(i, 2), :, :].rearrange("h r c -> r h c"))\
                      .then_inc(a_w[k2], 16)
                nodes(0, 0)
                nodes(1, 1)
                sp.wait_ge(s_split, 15)
                for n in range(3):
                    sp.dma_start(c2_three[n:n + 1, :], c2_parts[n][:, :]).then_inc(s_masks, 16)
                    for m in range(3):
                        sp.dma_start(w1w9[3 * m + n:3 * m + n + 1, :], w1w_parts[n][:, :]).then_inc(s_masks, 16)
                        sp.dma_start(w_d[:, 3 * n + m, :], w_parts[n][0:EQ, :]).then_inc(s_masks, 16)
                sp.wait_ge(s_masks, 16 * 24)
                steps(sp, EG, step)

            @block.vector
            def _(dve):
                q = slice(0, EQ)

                def finish(i, k, h):
                    k2 = k % 2
                    wait(dve, a_sd1, i + 1)
                    v.reciprocal(rs1[k2][:, :], sd1[k2][:, :]).then_inc(a_rs1, 1)
                    wait(dve, a_rs1, i + 1)
                    edge_rows = by_tile(xe[k], XW)
                    v.tensor_tensor(edge_rows[:, :, SCALE], rs1[k2][:, 0:J], dinv_t[:, cols(i, J)], ALU.mult)
                    v.tensor_copy(edge_rows[:, :, DINV], dinv_t[:, cols(i, J)]).then_inc(a_fe, 1)
                    for d in range(2):
                        v.tensor_copy(by_tile(x1n[2 * k2 + d], XW)[:, :, SCALE],
                                      rs1[k2][:, J + J * d:2 * J + J * d]).then_inc(a_fn, 1)

                def add_edges(i, k, h):
                    wait(dve, a_ue, i + 1)
                    wait(dve, a_put[k], 64 * h)
                    wait(dve, a_lin[k], 16 * h)
                    v.tensor_copy(put_idx[k][:, :], put_t[:, cols(i, J)]).then_inc(a_pi, 1)
                    v.tensor_tensor(by_tile(xe[k], XW)[:, :, 0:D], by_tile(BX[0], D),
                                    xg[k][:, G:2 * G].rearrange("p (j a) -> p j a", a=D),
                                    ALU.add).then_inc(a_ge, 1)

                def add_nodes(i, k, h):
                    for d in range(2):
                        k4 = 2 * (k % 2) + d
                        wait(dve, a_un, 2 * i + d + 1)
                        wait(dve, a_x1[k4], 16 * fill2(k, h))
                        v.tensor_tensor(by_tile(x1n[k4], XW)[:, :, 0:D], by_tile(BX[1 + d], D),
                                        by_tile(xn[2 * k + d], D), ALU.add).then_inc(a_ne, 1)

                def statistics1(i, k, h):
                    k2 = k % 2
                    parts = [by_tile(tile, XW) for tile in (xe[k], x1n[2 * k2], x1n[2 * k2 + 1])]
                    wait(dve, a_ge, i + 1)
                    wait(dve, a_ne, 2 * i + 2)
                    for n, tile in enumerate(parts):
                        for j in range(J):
                            last = v.bn_stats(st1[k2][:, J * n + j, :], tile[:, j, 0:D])
                    last.then_inc(a_st1, 1)
                    hold(dve, a_st1, i + 1)
                    for n, tile in enumerate(parts):
                        for j in range(J):
                            last = v.bn_aggr(tile[:, j, MEAN:MEAN + 2], st1[k2][:, J * n + j, :])
                    last.then_inc(a_mv1, 1)

                def scan_step(i, k, h):
                    wait(dve, a_ms, i + 1)
                    wait(dve, a_mask[k], 16 * h + 16)
                    wait(dve, a_pre, i - 1)
                    wait(dve, a_scan, i)
                    v.tensor_tensor_scan(
                        scan[k % 2][:, :], keepb[k][:, :], ms[k % 2][:, :],
                        -RESTART if isinstance(i, int) and i == 0 else scan[1 - k % 2][:, G - 1:G],
                        ALU.add, ALU.max).then_inc(a_scan, 1)

                def statistics(i, k, h):
                    k2 = k % 2
                    wait(dve, a_get[k], 128 * h + 128)
                    for j in range(2 * J):
                        v.bn_stats(st0[k2][:, j, :], xg[k][:, j * D:(j + 1) * D])
                    for d in range(2):
                        wait(dve, a_x[2 * k + d], 16 * h + 16)
                        for j in range(J):
                            last = v.bn_stats(st0[k2][:, 2 * J + J * d + j, :], xn[2 * k + d][:, j * D:(j + 1) * D])
                    last.then_inc(a_st, 1)

                def moments(i, k, h):
                    hold(dve, a_st, i + 1)
                    for j in range(4 * J):
                        last = v.bn_aggr(mv0[k % 2][:, j, :], st0[k % 2][:, j, :])
                    last.then_inc(a_mv, 1)

                def normalise(i, k, h):
                    k2 = k % 2
                    wait(dve, a_sd, i + 1)
                    v.reciprocal(rs0[k2][:, :], sd0[k2][:, :]).then_inc(a_rs, 1)
                    wait(dve, a_rs, i + 1)
                    wait(dve, a_nnorm, 2 * i - 2)
                    v.scalar_tensor_tensor(out=nb0[k2][:, :], in0=mv0[k2][:, J:4 * J, 0], scalar=-1.0,
                                           in1=rs0[k2][:, J:4 * J], op0=ALU.mult, op1=ALU.mult).then_inc(a_nb, 1)
                    for j in range(J):
                        row = xg[k][:, j * D:(j + 1) * D]
                        last = v.tensor_scalar(row, row, mv0[k2][:, j, 0:1], rs0[k2][:, j:j + 1],
                                               ALU.subtract, ALU.mult)
                    last.then_inc(a_norm, 1)

                def step(i, k, h):
                    if there(i):
                        normalise(i, k, h)
                    if there(back(2, i, k, h)[0]):
                        add_edges(*back(2, i, k, h))
                        add_nodes(*back(2, i, k, h))
                    if there(back(1, i, k, h)[0]):
                        scan_step(*back(1, i, k, h))
                    if there(back(-1, i, k, h)[0]):
                        statistics(*back(-1, i, k, h))
                    if there(back(-3, i, k, h)[0]):
                        place_indices(*back(-3, i, k, h)[:2])
                    if there(back(3, i, k, h)[0]):
                        finish(*back(3, i, k, h))
                    if there(back(-1, i, k, h)[0]):
                        moments(*back(-1, i, k, h))
                    if there(back(2, i, k, h)[0]):
                        statistics1(*back(2, i, k, h))
                v.memset(ones_bf[:, :], 1.0).then_inc(s_fill, 1)
                dve.wait_ge(s_weights, 16 * N_WEIGHTS)
                for n, (of, parts, rest) in enumerate((
                        (c2_row[:, :], [p[:, :] for p in c2_parts], [r[:, :] for r in rest_row]),
                        (w1w[:, :], [p[:, :] for p in w1w_parts], [r[:, 0:D] for r in rest_row]),
                        (w_a[q, :], [p[q, :] for p in w_parts], [r[q, :] for r in rest_a]))):
                    if n > 0:
                        dve.wait_ge(s_split, 5 * n)
                    v.tensor_copy(parts[0], of).then_inc(s_split, 1)
                    dve.wait_ge(s_split, 5 * n + 1)
                    v.tensor_tensor(rest[0], of, parts[0], ALU.subtract).then_inc(s_split, 1)
                    dve.wait_ge(s_split, 5 * n + 2)
                    v.tensor_copy(parts[1], rest[0]).then_inc(s_split, 1)
                    dve.wait_ge(s_split, 5 * n + 3)
                    v.tensor_tensor(rest[1], rest[0], parts[1], ALU.subtract).then_inc(s_split, 1)
                    dve.wait_ge(s_split, 5 * n + 4)
                    v.tensor_copy(parts[2], rest[1]).then_inc(s_split, 1)
                statistics(0, 0, 0)
                moments(0, 0, 0)
                steps(dve, EG, step, last=5)
                for i in range(EG, EG + 3):
                    step(i, i % 4, i // 4)

            @block.scalar
            def _(act):
                def deviations1(i, k, h):
                    k2 = k % 2
                    wait(act, a_mv1, i + 1)
                    wait(act, a_rs1, i - 1)
                    for n, tile in enumerate((xe[k], x1n[2 * k2], x1n[2 * k2 + 1])):
                        last = s.activation(sd1[k2][:, J * n:J * n + J], by_tile(tile, XW)[:, :, MEAN + 1], ACT.Sqrt,
                                            bias=eps_col[:, :])
                    last.then_inc(a_sd1, 1)

                def store(i, k, h):
                    wait(act, a_fe, i + 1)
                    act.dma_start(block_rows(xe_d, i), xe[k][:, :]).then_inc(a_lin[k], 16)
                    for d in range(2):
                        k4 = 2 * (k % 2) + d
                        wait(act, a_fn, 2 * i + d + 1)
                        if isinstance(i, int) and 2 * i + d == NG - 1:
                            act.wait_ge(a_x1[k4 - 1], 16 * (fill2(k, h) + 1))
                        act.dma_start(rows(x1_d, 2 * i + d, XW), x1n[k4][:, :]).then_inc(a_x1[k4], 16)

                def update_relu(i, k, h):
                    wait(act, a_pre, i + 1)
                    wait(act, a_ue, i - 1)
                    s.activation(zr[k % 2][:, :], BZ[:, :], ACT.Relu, bias=c1c[:, :]).then_inc(a_zr, 1)

                def deviations(i, k, h):
                    wait(act, a_mv, i + 1)
                    wait(act, a_rs, i - 1)
                    s.activation(sd0[k % 2][:, :], mv0[k % 2][:, :, 1], ACT.Sqrt, bias=eps_col[:, :]).then_inc(a_sd, 1)

                def normalise(to, of, k, first):
                    for j in range(J):
                        m = first + j
                        last = s.activation(to[:, j * D:(j + 1) * D], of[:, j * D:(j + 1) * D], ACT.Identity,
                                            bias=nb0[k % 2][:, m:m + 1], scale=rs0[k % 2][:, J + m:J + m + 1])
                    return last

                def node_normalise(i, k, d):
                    k4 = 2 * (k % 2) + d
                    wait(act, a_ntr, 2 * i + d - 3)
                    normalise(hn[k4], xn[2 * k + d], k, J + J * d).then_inc(a_nnorm, 1)

                def node_relu(i, k, d):
                    wait(act, a_ntr, 2 * i + d + 1)
                    wait(act, a_npre, 2 * i + d - 1)
                    s.activation(tn[d][:, :], BT[d][:, :], ACT.Relu).then_inc(a_ntn, 1)

                def node_hidden(i, k, d):
                    wait(act, a_npre, 2 * i + d + 1)
                    wait(act, a_un, 2 * i + d - 3)
                    s.activation(zn[2 * (k % 2) + d][:, :], (BN, BM)[d][:, :], ACT.Relu, bias=c1c[:, :]).then_inc(a_nzn, 1)

                def message_bias(i, k, h):
                    wait(act, a_msg, i + 1)
                    wait(act, a_scan, i - 1)
                    s.activation(ms[k % 2][:, :], BM[:, :], ACT.Identity, bias=b2c[:, :]).then_inc(a_ms, 1)

                def step(i, k, h):
                    k2 = k % 2
                    if there(back(1, i, k, h)[0]):
                        message_bias(*back(1, i, k, h))
                    if there(back(3, i, k, h)[0]):
                        deviations1(*back(3, i, k, h))
                    if there(i):
                        wait(act, a_nb, i + 1)
                        wait(act, a_tr, i - 1)
                        normalise(hg[k2], xg[k][:, G:2 * G], k, 0).then_inc(a_dnorm, 1)
                        node_normalise(i, k, 0)
                        wait(act, a_tr, i + 1)
                        wait(act, a_hid, i - 1)
                        s.activation(hs[k2][:, :], BT[0][:, :], ACT.Relu)
                        wait(act, a_pre, i - 3)
                        s.activation(hd[k][:, :], BT[1][:, :], ACT.Relu).then_inc(a_relu, 1)
                        node_normalise(i, k, 1)
                    if there(back(1, i, k, h)[0]):
                        node_hidden(*back(1, i, k, h)[:2], 0)
                        node_hidden(*back(1, i, k, h)[:2], 1)
                    if there(i):
                        wait(act, a_hid, i + 1)
                        wait(act, a_msg, i - 1)
                        s.activation(ze[k2][:, :], BZ[:, :], ACT.Relu, bias=b1c[:, :]).then_inc(a_ze, 1)
                    if there(i):
                        node_relu(i, k, 0)
                        node_relu(i, k, 1)
                    if there(back(-1, i, k, h)[0]):
                        deviations(*back(-1, i, k, h))
                    if there(back(1, i, k, h)[0]):
                        update_relu(*back(1, i, k, h))
                    if there(back(3, i, k, h)[0]):
                        store(*back(3, i, k, h))
                deviations(0, 0, 0)
                steps(act, EG, step)
                for i in range(EG, EG + 3):
                    step(i, i % 4, i // 4)
                for k in range(4):
                    act.wait_ge(a_x1[k], 16 * ((EG + 1 - k // 2) // 2))
                    act.wait_ge(a_lin[k], 16 * ((EG + 3 - k) // 4))

            @block.tensor
            def _(pe):
                def times_u2(to, of):
                    mm(to[:, :], ones_bf[:, :], c2_three[:, :], start=True, stop=False)
                    for j in range(J):
                        last = mm(to[:, j * D:(j + 1) * D], of[:, j * P:(j + 1) * P], u2[:, :],
                                  start=False, stop=j == J - 1)
                    return last

                def update(i, k, h):
                    k2 = k % 2
                    wait(pe, a_zr, i + 1)
                    wait(pe, a_ge, i)
                    times_u2(BX[0], zr[k2]).then_inc(a_ue, 1)
                    for d in range(2):
                        wait(pe, a_nzn, 2 * i + d + 1)
                        wait(pe, a_ne, 2 * i + d - 1)
                        times_u2(BX[1 + d], zn[2 * k2 + d]).then_inc(a_un, 1)

                def pre(i, k, h):
                    wait(pe, a_scan, i + 1)
                    wait(pe, a_ze, min(i + 2, EG) if isinstance(i, int) else i + 2)
                    mm(BZ[:, :], u1a[:, :], hd[k][:, :], start=True, stop=False)
                    mm(BZ[:, :], u1b[:, :], scan[k % 2][:, :], start=False, stop=True).then_inc(a_pre, 1)

                def node_transpose(i, k, d):
                    wait(pe, a_nnorm, 2 * i + d + 1)
                    wait(pe, a_relu, i + 1)
                    for j in range(J):
                        last = tr(BT[d][:, j * P:(j + 1) * P], hn[2 * (k % 2) + d][:, j * D:(j + 1) * D], ident[:, :])
                    last.then_inc(a_ntr, 1)

                def node_pre(i, d):
                    wait(pe, a_ntn, 2 * i + d + 1)
                    if d == 0:
                        wait(pe, a_nzn, 2 * i - 1)
                    else:
                        wait(pe, a_ms, i + 1)
                    mm((BN, BM)[d][:, :], u1a[:, :], tn[d][:, :], start=True, stop=True).then_inc(a_npre, 1)

                def step(i, k, h):
                    k2 = k % 2
                    if there(back(2, i, k, h)[0]):
                        update(*back(2, i, k, h))
                    if there(i):
                        wait(pe, a_norm, i + 1)
                        wait(pe, a_dnorm, i + 1)
                        wait(pe, a_ntn, 2 * i)
                        for n, tile in enumerate((xg[k], hg[k2])):
                            for j in range(J):
                                last = tr(BT[n][:, j * P:(j + 1) * P], tile[:, j * D:(j + 1) * D], ident[:, :])
                        last.then_inc(a_tr, 1)
                    if there(back(1, i, k, h)[0]):
                        for d in range(2):
                            node_pre(i - 1, d)
                    if there(i):
                        wait(pe, a_relu, i + 1)
                        wait(pe, a_w[k2], 16 * fill2(k, h) + 16)
                        wait(pe, a_zr, i - 1)
                        mm(BZ[:, :], w1w9[:, :], wrow[k2][:, :], start=True, stop=False)
                        mm(BZ[:, :], w1a[:, :], hs[k2][:, :], start=False, stop=False)
                        mm(BZ[:, :], w1b[:, :], hd[k][:, :], start=False, stop=True).then_inc(a_hid, 1)
                        node_transpose(i, k, 0)
                        node_transpose(i, k, 1)
                    if there(back(1, i, k, h)[0]):
                        pre(*back(1, i, k, h))
                    if there(i):
                        wait(pe, a_ze, i + 1)
                        wait(pe, a_nzn, 2 * i)
                        mm(BM[:, :], w2[:, :], ze[k2][:, :], start=True, stop=True).then_inc(a_msg, 1)
                steps(pe, EG, step)
                for i in range(EG, EG + 2):
                    step(i, i % 4, i // 4)

        setup_ctx.close()
        kept = xn + [sb(f"kept{n}", [P, G]) for n in range(3 * KEPT - len(xn))]

        def kept_tile(i, n):
            return kept[3 * (i - (EG - KEPT)) + n] if isinstance(i, int) and EG - KEPT <= i < EG else None

        b_get, b_mask, b_xe = (sems("b_" + n, 4) for n in ("get", "mask", "xe"))
        b_x = sems("b_x", 4)
        b_ae, b_an = sems("b_ae"), sems("b_an", 4)
        b_gi = sem("b_gi")
        b_norm, b_tr, b_relu, b_scan = (sem("b_" + n) for n in ("norm", "tr", "relu", "scan"))
        b_w = sem("b_w")
        b_wd = sem("b_wd")
        b_we = sem("b_we")
        b_act = sem("b_act")
        b_sc, b_nnorm, b_ntr, b_nrelu, b_nw, b_nb, b_nact = (
            sem("b_" + n) for n in ("sc", "nnorm", "ntr", "nrelu", "nw", "nb", "nact"))
        b_done = sem("b_done")
        BW, BD, BN = bank[2], bank[3:5], bank[5:7]

        with nc.Block() as block:
            @block.gpsimd
            def _(g):
                def step(i, k, h):
                    hold(g, b_tr, i - 3)
                    g.tensor_copy(get_idx[k][:, 0:J], src_t[:, cols(i, J)]).then_inc(b_gi, 1)
                    hold(g, b_gi, i + 1)
                    for j in range(J):
                        g.indirect_dma_start(
                            out=xg[k][:, j * XW:(j + 1) * XW], out_offset=None, in_=x1_d[:, :],
                            in_offset=bass.IndirectOffsetOnAxis(ap=get_idx[k][:, j:j + 1], axis=0),
                            bounds_check=N - 1, oob_is_err=False).then_inc(b_get[k], 16)
                steps(g, EG, step, 4, KEPT)

            @block.sync
            def _(sp):
                def step(i, k, h):
                    wait(sp, b_tr, i - 3)
                    sp.dma_start(xe[k][:, :], block_rows(xe_d, i)).then_inc(b_xe[k], 16)
                    wait(sp, b_scan, i - 3)
                    sp.dma_start(keepb[k][:, :], keep_d[cols(i, 1), :].to_broadcast([P, G])).then_inc(b_mask[k], 16)
                    wait(sp, b_wd, i - 3)
                    sp.dma_start(hd[k][:, :], share_d[cols(i, 1), :].to_broadcast([P, G])).then_inc(b_mask[k], 16)
                    for d in range(2):
                        wait(sp, b_ntr, 2 * i + d - 3)
                        sp.dma_start(x1n[2 * (k % 2) + d][:, :], rows(x1_d, 2 * i + d, XW))\
                          .then_inc(b_x[2 * (k % 2) + d], 16)
                steps(sp, EG, step, 4, KEPT)

            @block.vector
            def _(dve):
                def scan_step(i, k, h):
                    wait(dve, b_relu, i + 1)
                    wait(dve, b_mask[k], 32 * h + 32)
                    wait(dve, b_w, i - 1)
                    wait(dve, b_scan, i)
                    v.tensor_tensor_scan(
                        scan[k % 2][:, :], keepb[k][:, :], hs[k % 2][:, :],
                        0.0 if isinstance(i, int) and i == 0 else scan[1 - k % 2][:, G - 1:G],
                        ALU.mult, ALU.add).then_inc(b_scan, 1)

                def degree_step(i, k, h):
                    wait(dve, b_w, i + 1)
                    wait(dve, b_mask[k], 32 * h + 32)
                    wait(dve, b_we, i - 1)
                    v.tensor_tensor(ze[k % 2][:, :], BW[:, :], hd[k][:, :], ALU.mult).then_inc(b_wd, 1)

                def leaky(to, of):
                    return v.scalar_tensor_tensor(out=to[:, :], in0=of[:, :], scalar=SLOPE, in1=of[:, :],
                                                  op0=ALU.mult, op1=ALU.max)

                def statistics(slot, part):
                    to = stats[:, slot, :] if isinstance(slot, int) else stats[:, bass.ds(slot, 1), :]
                    return v.bn_stats(to, part)

                def activation(i, k, h):
                    k2 = k % 2
                    edges = kept_tile(i, 2) or zr[k2]
                    nodes = [kept_tile(i, d) or zn[2 * k2 + d] for d in range(2)]
                    wait(dve, b_we, i + 1)
                    if not kept_tile(i, 2):
                        wait(dve, b_ae[k2], 16 * fill2(k, h))
                    leaky(edges, ms[k2]).then_inc(b_act, 1)
                    for d in range(2):
                        wait(dve, b_nb, 2 * i + d + 1)
                        if not kept_tile(i, d):
                            wait(dve, b_an[2 * k2 + d], 16 * fill2(k, h))
                        leaky(nodes[d], hn[2 * k2 + d]).then_inc(b_nact, 1)
                    hold(dve, b_act, i + 1)
                    statistics(i + NG, edges[:, :])
                    hold(dve, b_nact, 2 * i + 2)
                    for d in range(2):
                        part = nodes[d][:, :]
                        if isinstance(i, int) and 2 * i + d == NG - 1:
                            part = part.rearrange("p (j q) -> p j q", j=J)[:, :, DOUBLE:P]
                        last = statistics(2 * i + d, part)
                    last.then_inc(b_done, 1)

                def normalise(i, k, h):
                    wait(dve, b_get[k], 64 * h + 64)
                    wait(dve, b_xe[k], 16 * h + 16)
                    for tile in (xg[k], xe[k]):
                        for j in range(J):
                            row, m = tile[:, j * XW:j * XW + D], j * XW + D
                            last = v.tensor_scalar(row, row, tile[:, m:m + 1], tile[:, m + 1:m + 2],
                                                   ALU.subtract, ALU.mult)
                    last.then_inc(b_norm, 1)

                def node_scales(i, k, h):
                    k2 = k % 2
                    wait(dve, b_nnorm, 2 * i - 2)
                    nodes = [by_tile(x1n[2 * k2 + d], XW) for d in range(2)]
                    for d in range(2):
                        wait(dve, b_x[2 * k2 + d], 16 * fill2(k, h) + 16)
                        v.scalar_tensor_tensor(out=rs1[k2][:, J * d:J * d + J], in0=nodes[d][:, :, DINV], scalar=1.0,
                                               in1=nodes[d][:, :, SCALE], op0=ALU.is_ge, op1=ALU.mult).then_inc(b_sc, 1)
                    wait(dve, b_sc, 4 * i + 2)
                    for d in range(2):
                        v.scalar_tensor_tensor(out=nb0[k2][:, J * d:J * d + J], in0=nodes[d][:, :, MEAN], scalar=-1.0,
                                               in1=rs1[k2][:, J * d:J * d + J], op0=ALU.mult,
                                               op1=ALU.mult).then_inc(b_sc, 1)

                def step(i, k, h):
                    if there(back(1, i, k, h)[0]):
                        scan_step(*back(1, i, k, h))
                    if there(i):
                        node_scales(i, k, h)
                    if there(back(-1, i, k, h)[0]):
                        normalise(*back(-1, i, k, h))
                    if there(back(1, i, k, h)[0]):
                        degree_step(*back(1, i, k, h))
                    if there(back(2, i, k, h)[0]):
                        activation(*back(2, i, k, h))
                normalise(0, 0, 0)
                steps(dve, EG, step, 4, KEPT)
                for i in range(EG, EG + 2):
                    step(i, i % 4, i // 4)

            @block.scalar
            def _(act):
                def edge_bias(i, k, h):
                    wait(act, b_wd, i + 1)
                    wait(act, b_act, i - 1)
                    s.activation(ms[k % 2][:, :], ze[k % 2][:, :], ACT.Identity, bias=biasc[:, :]).then_inc(b_we, 1)

                def store_edges(i, k, h):
                    wait(act, b_act, i + 1)
                    act.dma_start(block_rows(acte_d, i), zr[k % 2][:, :]).then_inc(b_ae[k % 2], 16)

                def store_nodes(i, k, h):
                    for d in range(2):
                        k4 = 2 * (k % 2) + d
                        wait(act, b_nact, 2 * i + d + 1)
                        act.dma_start(block_rows(act_d, 2 * i + d), zn[k4][:, :]).then_inc(b_an[k4], 16)

                def step(i, k, h):
                    k2 = k % 2
                    if there(back(2, i, k, h)[0]):
                        edge_bias(*back(2, i, k, h))
                    if there(back(1, i, k, h)[0]):
                        for d in range(2):
                            wait(act, b_ntr, 2 * (i - 1) + d + 1)
                            wait(act, b_nw, 2 * (i - 1) + d - 1)
                            s.activation(tn[d][:, :], BD[d][:, :], ACT.Relu).then_inc(b_nrelu, 1)
                    if there(i):
                        wait(act, b_tr, i + 1)
                        wait(act, b_scan, i - 1)
                        s.activation(hs[k2][:, :], bank[0][:, :], ACT.Relu)
                        wait(act, b_w, i - 1)
                        s.activation(hg[k2][:, :], bank[1][:, :], ACT.Relu).then_inc(b_relu, 1)
                        wait(act, b_sc, 4 * i + 4)
                        for d in range(2):
                            x1 = by_tile(x1n[2 * k2 + d], XW)
                            for j in range(J):
                                m = J * d + j
                                last = s.activation(x1[:, j, 0:D], x1[:, j, 0:D], ACT.Identity,
                                                    bias=nb0[k2][:, m:m + 1], scale=rs1[k2][:, m:m + 1])
                            last.then_inc(b_nnorm, 1)
                    if there(back(1, i, k, h)[0]):
                        for d in range(2):
                            b = back(1, i, k, h)
                            wait(act, b_nw, 2 * b[0] + d + 1)
                            wait(act, b_nact, 2 * b[0] + d - 3)
                            s.activation(hn[2 * (b[1] % 2) + d][:, :], BN[d][:, :], ACT.Identity,
                                         bias=biasc[:, :]).then_inc(b_nb, 1)
                    if there(back(2, i, k, h)[0]) and not kept_tile(back(2, i, k, h)[0], 0):
                        store_edges(*back(2, i, k, h))
                        store_nodes(*back(2, i, k, h))
                steps(act, EG, step, 4, KEPT)
                for i in range(EG, EG + 2):
                    step(i, i % 4, i // 4)
                for k in range(4):
                    act.wait_ge(b_an[k], 16 * ((EG - KEPT + 1 - k // 2) // 2))
                for k in range(2):
                    act.wait_ge(b_ae[k], 16 * ((EG - KEPT + 1 - k) // 2))

            @block.tensor
            def _(pe):
                def times_w(i, k, h):
                    wait(pe, b_scan, i + 1)
                    wait(pe, b_wd, i)
                    mm(BW[:, :], wg[:, :], hg[k % 2][:, :], start=True, stop=False)
                    mm(BW[:, :], wg[:, :], scan[k % 2][:, :], start=False, stop=True).then_inc(b_w, 1)

                def node_transposes(i, k, h):
                    for d in range(2):
                        wait(pe, b_nnorm, 2 * i + d + 1)
                        wait(pe, b_nrelu, 2 * i + d - 1)
                        for j in range(J):
                            last = tr(BD[d][:, j * P:(j + 1) * P], x1n[2 * (k % 2) + d][:, j * XW:j * XW + D],
                                      ident[:, :])
                        last.then_inc(b_ntr, 1)

                def step(i, k, h):
                    if there(back(1, i, k, h)[0]):
                        node_transposes(*back(1, i, k, h))
                    if there(i):
                        wait(pe, b_norm, i + 1)
                        wait(pe, b_relu, i)
                        for n, tile in enumerate((xg[k], xe[k])):
                            for j in range(J):
                                last = tr(bank[n][:, j * P:(j + 1) * P], tile[:, j * XW:j * XW + D], ident[:, :])
                        last.then_inc(b_tr, 1)
                    if there(back(1, i, k, h)[0]):
                        times_w(*back(1, i, k, h))
                        for d in range(2):
                            wait(pe, b_nrelu, 2 * (i - 1) + d + 1)
                            wait(pe, b_nb, 2 * (i - 1) + d - 1)
                            mm(BN[d][:, :], wg[:, :], tn[d][:, :], start=True, stop=True).then_inc(b_nw, 1)
                steps(pe, EG, step, 4, KEPT)
                step(EG, EG % 4, EG // 4)

        o_chain, o_std, o_coef = sem("o_chain"), sem("o_std"), sem("o_coef")
        o_ld = [sems(f"o_ld{n}_", 4) for n in range(3)]
        o_st = sems("o_st", 4)
        o_put = sems("o_put", 4)
        o_pi = sem("o_pi")
        o_keep = sem("o_keep")
        o_late = sem("o_late")
        o_y, o_tr, o_sum = sem("o_y"), sem("o_tr"), sem("o_sum")
        small = {n: sb(n, [P, w_]) for n, w_ in (
            ("moments", 2), ("fill0", 1), ("fill", 1), ("off", 1), ("off2", 1), ("more", 1), ("mean", 1),
            ("dist", 1), ("dist2", 1), ("spread", 1), ("var", 1), ("std", 1), ("inv", 1), ("scale", 1),
            ("prod", 1), ("shift", 1))}
        NE = EG * G
        NALL = N + NE
        oa = [hd, ms + scan, keepb]
        ox = [x1n, xe, [tile[:, 0:J * XW] for tile in xg]]

        def loaded(i, h):
            return 32 * h + 32 if not kept_tile(i, 0) else 16 * ((EG - KEPT) // 4 + h + 1)

        oy = [hs, hg, ze]
        oo = zn

        with nc.Block() as block:
            @block.gpsimd
            def _(g):
                def scatter(i, k, h):
                    hold(g, o_put[k], 64 * h)
                    g.tensor_copy(put_idx[k][:, :], put_t[:, cols(i, J)]).then_inc(o_pi, 1)
                    hold(g, o_pi, i + 1)
                    hold(g, o_sum, 3 * i + 3)
                    with g.If(late > 0):
                        g.dma_start(block_rows(acte_d, i), hn[k][:, :]).then_inc(o_keep, 16)
                        hold(g, o_keep, 16 * i + 16)
                    for d in range(2):
                        hold(g, o_st[2 * (k % 2) + d], 16 * fill2(k, h) + 16)
                    for j in range(J):
                        g.indirect_dma_start(
                            out=out[:, :], in_=hn[k][:, j * D:(j + 1) * D],
                            out_offset=bass.IndirectOffsetOnAxis(ap=put_idx[k][:, j:j + 1], axis=0),
                            in_offset=None, bounds_check=N - 1, oob_is_err=False).then_inc(o_put[k], 16)
                g.wait_ge(s_flag, 4)
                late = g.value_load(any_late[0:1, 0:1])
                steps(g, EG, scatter, 4, KEPT)
                for k in range(4):
                    g.wait_ge(o_put[k], 64 * ((EG + 3 - k) // 4))
                    g.wait_ge(o_st[k], 16 * ((EG + 1 - k // 2) // 2))
                late_rows(g, out, acte_d, D, hn[0], o_late, o_pi)

            @block.sync
            def _(sp):
                def step(i, k, h):
                    for n in range(3):
                        if not kept_tile(i, n):
                            wait(sp, o_y, 3 * (i - 4) + n + 1)
                            a = block_rows(act_d, 2 * i + n) if n < 2 else block_rows(acte_d, i)
                            sp.dma_start(oa[n][k][:, :], a).then_inc(o_ld[n][k], 16)
                        wait(sp, o_sum, 3 * (i - 4) + n + 1)
                        r = rows(x1_d, 2 * i + n, XW) if n < 2 else block_rows(xe_d, i)
                        sp.dma_start(ox[n][k][:, :], r).then_inc(o_ld[n][k], 16)
                steps(sp, EG, step, 4, KEPT)

            @block.vector
            def _(dve):
                c = {n: tile[:, :] for n, tile in small.items()}
                count = [0]

                def chained(instruction):
                    count[0] += 1
                    instruction.then_inc(o_chain, 1)
                    dve.wait_ge(o_chain, count[0])

                chained(v.bn_aggr(c["moments"], stats[:, :, :].rearrange("p t s -> p (t s)")))
                chained(v.tensor_scalar(c["fill0"], biasc[:, :], SLOPE, None, ALU.mult))
                chained(v.tensor_tensor(c["fill"], c["fill0"], biasc[:, :], ALU.max))
                chained(v.tensor_tensor(c["off"], small["moments"][:, 0:1], c["fill"], ALU.subtract))
                chained(v.scalar_tensor_tensor(out=c["mean"], in0=c["off"], scalar=NALL / N, in1=c["fill"],
                                               op0=ALU.mult, op1=ALU.add))
                chained(v.tensor_tensor(c["dist"], small["moments"][:, 0:1], c["mean"], ALU.subtract))
                chained(v.tensor_tensor(c["dist2"], c["dist"], c["dist"], ALU.mult))
                chained(v.tensor_tensor(c["spread"], c["dist2"], small["moments"][:, 1:2], ALU.add))
                chained(v.tensor_tensor(c["off"], c["fill"], c["mean"], ALU.subtract))
                chained(v.tensor_tensor(c["off2"], c["off"], c["off"], ALU.mult))
                chained(v.tensor_scalar(c["more"], c["off2"], NE / N, None, ALU.mult))
                chained(v.scalar_tensor_tensor(out=c["var"], in0=c["spread"], scalar=NALL / N, in1=c["more"],
                                               op0=ALU.mult, op1=ALU.subtract))
                dve.wait_ge(o_std, 1)
                chained(v.reciprocal(c["inv"], c["std"]))
                chained(v.tensor_tensor(c["scale"], gammac[:, :], c["inv"], ALU.mult))
                chained(v.tensor_tensor(c["prod"], c["mean"], c["scale"], ALU.mult))
                v.tensor_tensor(c["shift"], betac[:, :], c["prod"], ALU.subtract).then_inc(o_coef, 1)

                def step(i, k, h):
                    for n in range(3):
                        wait(dve, o_tr, 3 * i + n + 1)
                        wait(dve, o_ld[n][k], loaded(i, h))
                        if n < 2:
                            k4 = 2 * (k % 2) + n
                            wait(dve, o_st[k4], 16 * fill2(k, h))
                            to = oo[k4]
                        else:
                            wait(dve, o_put[k], 64 * h)
                            to = hn[k]
                        last = v.tensor_tensor(by_tile(to, D), by_tile(bank[(3 * k + n) % 6], D),
                                               by_tile(ox[n][k], XW)[:, :, 0:D], ALU.add)
                        last.then_inc(o_sum, 1)
                steps(dve, EG, step, 4, KEPT)

            @block.scalar
            def _(act):
                act.wait_ge(o_chain, 12)
                s.activation(small["std"][:, :], small["var"][:, :], ACT.Sqrt, bias=eps_col[:, :]).then_inc(o_std, 1)
                act.wait_ge(o_coef, 1)

                def store(i, k, h):
                    for n in range(2):
                        k4 = 2 * (k % 2) + n
                        wait(act, o_sum, 3 * i + n + 1)
                        if isinstance(i, int) and 2 * i + n == NG - 1:
                            act.wait_ge(o_st[k4 - 1], 16 * (fill2(k, h) + 1))
                        act.dma_start(rows(out, 2 * i + n, D), oo[k4][:, :]).then_inc(o_st[k4], 16)

                def step(i, k, h):
                    for n in range(3):
                        y = oy[n][k % 2]
                        if not kept_tile(i, n):
                            wait(act, o_ld[n][k], loaded(i, h))
                        wait(act, o_tr, 3 * (i - 2) + n + 1)
                        s.activation(y[:, :], (kept_tile(i, n) or oa[n][k])[:, :], ACT.Identity, bias=small["shift"][:, :],
                                     scale=small["scale"][:, :]).then_inc(o_y, 1)
                    if there(back(1, i, k, h)[0]):
                        store(*back(1, i, k, h))
                steps(act, EG, step, 4, KEPT)
                store(EG - 1, (EG - 1) % 4, (EG - 1) // 4)
                for k in range(4):
                    act.wait_ge(o_st[k], 16 * ((EG + 1 - k // 2) // 2))

            @block.tensor
            def _(pe):
                def step(i, k, h):
                    for n in range(3):
                        wait(pe, o_y, 3 * i + n + 1)
                        wait(pe, o_sum, 3 * (i - 2) + n + 1)
                        for j in range(J):
                            last = tr(bank[(3 * k + n) % 6][:, j * D:(j + 1) * D],
                                      oy[n][k % 2][:, j * P:(j + 1) * P], ident[:, :])
                        last.then_inc(o_tr, 1)
                steps(pe, EG, step, 4, KEPT)


_INPUTS = ["x", "src", "dst", "edge_weight", "L0_gnn_W1", "L0_gnn_b1", "L0_gnn_W2", "L0_gnn_b2", "L0_gnn_U1",
           "L0_gnn_c1", "L0_gnn_U2", "L0_gnn_c2", "L1_gnn_W", "L1_gnn_bias", "L1_gnn_gamma", "L1_gnn_beta"]


def kernel(**inputs):
    import numpy as np
    import concourse.bacc as bacc
    from concourse import mybir as mb
    from concourse.bass_utils import run_bass_kernel_spmd

    nc = bacc.Bacc("TRN2", target_bir_lowering=False, num_devices=1)
    arrays, args = {}, []
    for name in _INPUTS:
        a = np.ascontiguousarray(inputs[name])
        arrays[f"in_{name}"] = a
        args.append(nc.dram_tensor(f"in_{name}", a.shape, mb.dt.from_np(a.dtype), kind="ExternalInput").ap())
    out = nc.dram_tensor("out_x", arrays["in_x"].shape, mb.dt.float32, kind="ExternalOutput").ap()
    gnn_kernel(nc, *args, out)
    r = run_bass_kernel_spmd(nc, [arrays], core_ids=[0])
    return r.results[0]["out_x"]
```
